# Optimizing a Trainium2 kernel written in Bass

```python
import numpy as np
import jax
import jax.numpy as jnp

def _softmax(x, axis=-1):
    return jax.nn.softmax(x, axis=axis)

def _gelu(x):
    return jax.nn.gelu(x, approximate=True)

def _silu(x):
    return jax.nn.silu(x)

def _sigmoid(x):
    return jax.nn.sigmoid(x)

def _layernorm(x, axis=-1, eps=1e-05):
    m = jnp.mean(x, axis=axis, keepdims=True)
    v = jnp.var(x, axis=axis, keepdims=True)
    return (x - m) / jnp.sqrt(v + eps)

def _scatter_add(tgt, idx, src, axis=0):
    return tgt.at[idx].add(src)

def _segment_sum(src, seg, n):
    return jax.ops.segment_sum(src, seg, n)
kernel_name = 'mk_adaln_d1_jaxref_r8_cd9d0f'

def setup_inputs(seed: int=0):
    np.random.seed(seed)
    _w = jnp.asarray

    def _L0_attn_setup():
        import jax, jax.numpy as jnp
        import numpy as np
        B, T, D_MODEL = (4, 512, 256)
        D_LATENT = 64
        D_COMP = 32
        THETA = 10000.0
        LN_EPS = 1e-05

        def _rope_tables(seq_len: int, dim: int):
            inv_freq = 1.0 / THETA ** (jnp.arange(0, dim, 2, dtype=jnp.float32) / dim)
            freqs = jnp.arange(seq_len, dtype=jnp.float32)[:, None] * inv_freq[None, :]
            cos = jnp.concatenate([jnp.cos(freqs), jnp.cos(freqs)], axis=-1)
            sin = jnp.concatenate([jnp.sin(freqs), jnp.sin(freqs)], axis=-1)
            return (cos, sin)

        def _rotate_half(x):
            x1, x2 = jnp.split(x, 2, axis=-1)
            return jnp.concatenate([-x2, x1], axis=-1)
        key = jax.random.key(seed)
        ks = jax.random.split(key, 8)
        s = 0.02
        return {'x': jax.random.normal(ks[0], (B, T, D_MODEL), dtype=jnp.float32), 'W_to_kv': jax.random.normal(ks[1], (D_LATENT, D_MODEL), dtype=jnp.float32) * s, 'W_compress': jax.random.normal(ks[2], (D_COMP, D_LATENT), dtype=jnp.float32) * s, 'ln_gamma': jnp.ones((D_COMP,), dtype=jnp.float32), 'ln_beta': jnp.zeros((D_COMP,), dtype=jnp.float32), 'W_q_comp': jax.random.normal(ks[3], (D_COMP, D_COMP), dtype=jnp.float32) * s, 'W_kv_comp': jax.random.normal(ks[4], (2 * D_COMP, D_COMP), dtype=jnp.float32) * s, 'W_comp2lat': jax.random.normal(ks[5], (D_LATENT, D_COMP), dtype=jnp.float32) * s, 'W_out_res': jnp.zeros((D_MODEL, D_LATENT), dtype=jnp.float32), 'b_out_res': jnp.zeros((D_MODEL,), dtype=jnp.float32)}
    _L0_attn_in = _L0_attn_setup()

    def _L0_ffn_setup():
        import jax, jax.numpy as jnp
        import numpy as np
        BLOCK_SIZE = 32
        HIDDEN_SIZE = 256
        MLP_DIM = 2048
        NVFP4_LUT = jnp.array([0.0, 0.5, 1.0, 1.5, 2.0, 3.0, 4.0, 6.0, 0.0, -0.5, -1.0, -1.5, -2.0, -3.0, -4.0, -6.0], dtype=jnp.float32)

        def dequant_nvfp4(W_packed, scales, block=BLOCK_SIZE):
            N = W_packed.shape[0]
            low = W_packed & 15
            high = W_packed >> 4 & 15
            idx = jnp.stack([low, high], axis=-1).reshape(N, -1)
            vals = NVFP4_LUT[idx]
            K = vals.shape[1]
            vals = vals.reshape(N, K // block, block) * scales[:, :, None]
            return vals.reshape(N, K)
        key = jax.random.key(seed)
        ks = jax.random.split(key, 7)
        x = jax.random.normal(ks[0], (4, 32, HIDDEN_SIZE), dtype=jnp.float32)
        gate_W_packed = jax.random.randint(ks[1], (MLP_DIM, HIDDEN_SIZE // 2), 0, 32, dtype=jnp.int32)
        gate_scales = jax.random.uniform(ks[2], (MLP_DIM, HIDDEN_SIZE // BLOCK_SIZE), dtype=jnp.float32) * 0.1 + 0.001
        up_W_packed = jax.random.randint(ks[3], (MLP_DIM, HIDDEN_SIZE // 2), 0, 32, dtype=jnp.int32)
        up_scales = jax.random.uniform(ks[4], (MLP_DIM, HIDDEN_SIZE // BLOCK_SIZE), dtype=jnp.float32) * 0.1 + 0.001
        down_W_packed = jax.random.randint(ks[5], (HIDDEN_SIZE, MLP_DIM // 2), 0, 32, dtype=jnp.int32)
        down_scales = jax.random.uniform(ks[6], (HIDDEN_SIZE, MLP_DIM // BLOCK_SIZE), dtype=jnp.float32) * 0.1 + 0.001
        return {'x': x, 'gate_W_packed': gate_W_packed, 'gate_scales': gate_scales, 'up_W_packed': up_W_packed, 'up_scales': up_scales, 'down_W_packed': down_W_packed, 'down_scales': down_scales}
    _L0_ffn_in = _L0_ffn_setup()
    _L0_c = _w((lambda *s: np.random.randn(*s).astype(np.float32) * 0.05)(1, 256))
    _L0_wmod = _w((lambda *s: np.random.randn(*s).astype(np.float32) * 0.05)(256, 6 * 256) * 256 ** (-0.5))
    _d = {'L0_attn_x': _L0_attn_in['x'], 'L0_attn_W_to_kv': _L0_attn_in['W_to_kv'], 'L0_attn_W_compress': _L0_attn_in['W_compress'], 'L0_attn_ln_gamma': _L0_attn_in['ln_gamma'], 'L0_attn_ln_beta': _L0_attn_in['ln_beta'], 'L0_attn_W_q_comp': _L0_attn_in['W_q_comp'], 'L0_attn_W_kv_comp': _L0_attn_in['W_kv_comp'], 'L0_attn_W_comp2lat': _L0_attn_in['W_comp2lat'], 'L0_attn_W_out_res': _L0_attn_in['W_out_res'], 'L0_attn_b_out_res': _L0_attn_in['b_out_res'], 'L0_ffn_gate_W_packed': _L0_ffn_in['gate_W_packed'], 'L0_ffn_gate_scales': _L0_ffn_in['gate_scales'], 'L0_ffn_up_W_packed': _L0_ffn_in['up_W_packed'], 'L0_ffn_up_scales': _L0_ffn_in['up_scales'], 'L0_ffn_down_W_packed': _L0_ffn_in['down_W_packed'], 'L0_ffn_down_scales': _L0_ffn_in['down_scales'], 'L0_c': _L0_c, 'L0_wmod': _L0_wmod}
    _x0 = _d['L0_attn_x']
    _d['L0_attn_x'] = jax.random.normal(jax.random.fold_in(jax.random.key(seed), 1), (1, 1024, 256), dtype=_x0.dtype)
    del _x0
    return _d

def reference(L0_attn_x, L0_attn_W_to_kv, L0_attn_W_compress, L0_attn_ln_gamma, L0_attn_ln_beta, L0_attn_W_q_comp, L0_attn_W_kv_comp, L0_attn_W_comp2lat, L0_attn_W_out_res, L0_attn_b_out_res, L0_ffn_gate_W_packed, L0_ffn_gate_scales, L0_ffn_up_W_packed, L0_ffn_up_scales, L0_ffn_down_W_packed, L0_ffn_down_scales, L0_c, L0_wmod):

    def _L0_attn_ref(x, W_to_kv, W_compress, ln_gamma, ln_beta, W_q_comp, W_kv_comp, W_comp2lat, W_out_res, b_out_res):
        import jax, jax.numpy as jnp
        import numpy as np
        B, T, D_MODEL = (4, 512, 256)
        D_LATENT = 64
        D_COMP = 32
        THETA = 10000.0
        LN_EPS = 1e-05

        def _rope_tables(seq_len: int, dim: int):
            inv_freq = 1.0 / THETA ** (jnp.arange(0, dim, 2, dtype=jnp.float32) / dim)
            freqs = jnp.arange(seq_len, dtype=jnp.float32)[:, None] * inv_freq[None, :]
            cos = jnp.concatenate([jnp.cos(freqs), jnp.cos(freqs)], axis=-1)
            sin = jnp.concatenate([jnp.sin(freqs), jnp.sin(freqs)], axis=-1)
            return (cos, sin)

        def _rotate_half(x):
            x1, x2 = jnp.split(x, 2, axis=-1)
            return jnp.concatenate([-x2, x1], axis=-1)
        Bx, Tx, _ = x.shape
        dc = W_compress.shape[0]
        kv_latent = x @ W_to_kv.T
        c = kv_latent @ W_compress.T
        mu = jnp.mean(c, axis=-1, keepdims=True)
        var = jnp.mean((c - mu) ** 2, axis=-1, keepdims=True)
        ch = (c - mu) * jax.lax.rsqrt(var + LN_EPS) * ln_gamma + ln_beta
        q = ch @ W_q_comp.T
        kv = ch @ W_kv_comp.T
        k, v = jnp.split(kv, 2, axis=-1)
        cos, sin = _rope_tables(Tx, dc)
        q = q * cos + _rotate_half(q) * sin
        k = k * cos + _rotate_half(k) * sin
        scale = 1.0 / jnp.sqrt(jnp.float32(dc))
        scores = jnp.einsum('btd,bsd->bts', q, k) * scale
        causal = jnp.tril(jnp.ones((Tx, Tx), dtype=bool))
        scores = jnp.where(causal[None], scores, jnp.float32(-1e+30))
        attn = jax.nn.softmax(scores, axis=-1)
        o = jnp.einsum('bts,bsd->btd', attn, v)
        z = o @ W_comp2lat.T
        out = z @ W_to_kv + z @ W_out_res.T + b_out_res
        return out

    def _L0_ffn_ref(x, gate_W_packed, gate_scales, up_W_packed, up_scales, down_W_packed, down_scales):
        import jax, jax.numpy as jnp
        import numpy as np
        BLOCK_SIZE = 32
        HIDDEN_SIZE = 256
        MLP_DIM = 2048
        NVFP4_LUT = jnp.array([0.0, 0.5, 1.0, 1.5, 2.0, 3.0, 4.0, 6.0, 0.0, -0.5, -1.0, -1.5, -2.0, -3.0, -4.0, -6.0], dtype=jnp.float32)

        def dequant_nvfp4(W_packed, scales, block=BLOCK_SIZE):
            N = W_packed.shape[0]
            low = W_packed & 15
            high = W_packed >> 4 & 15
            idx = jnp.stack([low, high], axis=-1).reshape(N, -1)
            vals = NVFP4_LUT[idx]
            K = vals.shape[1]
            vals = vals.reshape(N, K // block, block) * scales[:, :, None]
            return vals.reshape(N, K)
        B, S, H = x.shape
        xt = x.reshape(B * S, H)
        Wg = dequant_nvfp4(gate_W_packed, gate_scales)
        Wu = dequant_nvfp4(up_W_packed, up_scales)
        Wd = dequant_nvfp4(down_W_packed, down_scales)
        gate = jnp.einsum('th,nh->tn', xt, Wg)
        up = jnp.einsum('th,nh->tn', xt, Wu)
        gelu = jnp.tanh(0.7978845608028654 * (gate + 0.044715 * gate ** 3)) * gate * 0.5 + gate * 0.5
        inter = gelu * up
        out = jnp.einsum('tn,hn->th', inter, Wd)
        return out.reshape(B, S, H)
    x = L0_attn_x
    mod = (_silu(L0_c) @ L0_wmod).reshape(L0_c.shape[0], 6, 1, -1)
    sa, ca, ga, sb, cb, gb = (mod[:, 0], mod[:, 1], mod[:, 2], mod[:, 3], mod[:, 4], mod[:, 5])
    ga = (2 * (ga >= 0) - 1) * jnp.maximum(jnp.abs(ga), 0.25)
    gb = (2 * (gb >= 0) - 1) * jnp.maximum(jnp.abs(gb), 0.25)
    h = _layernorm(x, axis=-1) * (1 + ca) + sa
    x = x + ga * _L0_attn_ref(h, L0_attn_W_to_kv, L0_attn_W_compress, L0_attn_ln_gamma, L0_attn_ln_beta, L0_attn_W_q_comp, L0_attn_W_kv_comp, L0_attn_W_comp2lat, L0_attn_W_out_res, L0_attn_b_out_res)
    h = _layernorm(x, axis=-1) * (1 + cb) + sb
    x = x + gb * _L0_ffn_ref(h, L0_ffn_gate_W_packed, L0_ffn_gate_scales, L0_ffn_up_W_packed, L0_ffn_up_scales, L0_ffn_down_W_packed, L0_ffn_down_scales)
    return x

_drawn_inputs = setup_inputs


def setup_inputs(seed=0):
    import zlib

    import numpy as np

    out = dict(_drawn_inputs(seed))
    spreads = {'L0_attn_ln_gamma': (1.0, 0.6),
     'L0_attn_ln_beta': (0.0, 0.8),
     'L0_attn_W_out_res': (0.0, 0.8),
     'L0_attn_b_out_res': (0.0, 0.267)}
    factors = {'L0_attn_W_to_kv': 8.0,
     'L0_attn_W_compress': 8.0,
     'L0_attn_W_q_comp': 8.0,
     'L0_attn_W_kv_comp': 8.0,
     'L0_attn_W_comp2lat': 8.0}
    for name, (base, spread) in spreads.items():
        noise = np.random.default_rng([zlib.crc32(name.encode()), seed]).standard_normal(out[name].shape)
        drawn = base * np.exp(spread * noise) if base else spread * noise
        out[name] = jnp.asarray(drawn.astype(out[name].dtype))
    for name, factor in factors.items():
        out[name] = (out[name] * factor).astype(out[name].dtype)
    return out
```

```python
from contextlib import ExitStack

import numpy as np

import concourse.bass as bass
from concourse import mybir
from concourse.alu_op_type import AluOpType as ALU

ACT = mybir.ActivationFunctionType
AX_X = mybir.AxisListType.X
F32 = mybir.dt.float32
F32R = mybir.dt.float32r
F16 = mybir.dt.float16
BF16 = mybir.dt.bfloat16
I32 = mybir.dt.int32

P = 128
T, D = 1024, 256
DLAT, DC = 64, 32
FF = 2048
TILES = T // P
HALF = 512
HT = HALF // P
KT = D // P
GROUPS = FF // (2 * P)
UNITS = 2 * GROUPS
WORDS = 3 * 2 * P
BLOCK = 32
REP = BLOCK // 2
EPS = 1e-5
SCALE = float(1.0 / np.sqrt(np.float32(DC)))
RSQRT_SEED = float(0x5F3759DF)
FP16_BIAS = 2.0 ** 14

C_ID, C_SELQ, C_SELK, C_MASK, C_QM, C_KM, C_N = 0, P, 2 * P, 3 * P, 4 * P, 4 * P + 1, 4 * P + 2
A_KV, A_OUT, A_LAT, A_CMP, A_N = 0, D, 2 * D, 2 * D + 2 * DC, 2 * D + 3 * DC
B_QK, B_V, B_GAMMA, B_BETA, B_N = 0, 4 * DC, 5 * DC, 5 * DC + 1, 5 * DC + 2
SA, CA, GA, SB, CB, GB = range(6)
M_SA, M_CA, M_SB, M_CB, M_GB = 0, 2, 4, 6, 8


def build_block(nc, x, wmod, c_col, attn64, attn32, b_out, consts, rope, packed, scales, out):
    with ExitStack() as ctx:
        def sb(name, shape, dt=F32):
            return ctx.enter_context(nc.sbuf_tensor(name, shape, dt))

        def sem(name):
            return ctx.enter_context(nc.semaphore(name))

        ps = ctx.enter_context(nc.psum_tensor("ps", [P, 8, 512], F32))
        flat = ps[:].rearrange("p b n -> p (b n)")
        S0, PT0 = 0, 2
        GATE, UP, YT = 4, 5, 6

        xres = sb("xres", [P, TILES, D])
        wmod_sb = sb("wmod_sb", [P, KT, 6 * D])
        c_sb = sb("c_sb", [P, KT])
        a64 = sb("a64", [DLAT, A_N])
        a32 = sb("a32", [DC, B_N])
        bout_sb = sb("bout_sb", [P, D])
        cst = sb("cst", [P, C_N])
        rope_sb = sb("rope_sb", [P, T])
        wbuf = sb("wbuf", [P, GROUPS, 2, WORDS])

        identb = sb("identb", [P, P], BF16)
        maskb = sb("maskb", [P, P], BF16)
        silu_t = sb("silu_t", [P, 3, KT])
        silu = sb("silu", [P, KT])
        mods = sb("mods", [P, 10])
        ga_t = sb("ga_t", [P, 2, D])
        ga_b = sb("ga_b", [P, D])
        gab = sb("gab", [P, D])
        gb_t = sb("gb_t", [P, 2, KT])
        wsum = sb("wsum", [DLAT, D])
        wo = sb("wo", [2 * DC, D])
        wc_mean = sb("wc_mean", [P, KT])
        wcc = sb("wcc", [P, KT, DC])
        wcm = sb("wcm", [P, KT, DC])
        cbias = sb("cbias", [P, DC])

        stats = sb("stats", [P, TILES, 6])
        mv = sb("mv", [P, TILES, 2])
        rs_v = sb("rs_v", [P, HT])
        rs_y = sb("rs_y", [P, HT])
        rs_t = sb("rs_t", [P, HT])
        xn = sb("xn", [P, HT, D])
        xnT = sb("xnT", [P, KT, HALF])
        cc = sb("cc", [P, HT, DC])
        csq = sb("csq", [P, HT, DC])
        cvar = sb("cvar", [P, HT])
        chT = sb("chT", [DC, HALF])
        prod = sb("prod", [P, HALF])
        hi_t = sb("hi_t", [P, 2, HALF], F32R)
        QS = sb("QS", [P, HALF], F32R)
        KS = sb("KS", [P, T], F32R)
        VS = sb("VS", [P, TILES, 2 * DC], F32R)
        nmax = sb("nmax", [P, TILES])
        nbias = sb("nbias", [P, TILES])
        den = sb("den", [P, TILES])
        rden = sb("rden", [P, TILES])
        probs = sb("probs", [P, T])
        PS12 = sb("PS12", [P, 2, T], F32R)
        oT = sb("oT", [2 * DC, P])
        hfull = sb("hfull", [P, 2, HALF])
        H = sb("H", [P, 2, 2, 2, HALF], F32R)

        dec_a = sb("dec_a", [P, WORDS], I32)
        dec_b = sb("dec_b", [P, WORDS], I32)
        dec_v = sb("dec_v", [P, WORDS], I32)
        WS = sb("WS", [P, 2, 2, 2, 3, 2 * P], F32R)
        gel = sb("gel", [P, 2, HALF])
        inter = sb("inter", [P, 2, HALF])
        IS = sb("IS", [P, 2, 2, HALF], F32R)
        yT = sb("yT", [P, KT, HALF])

        ident = cst[:, C_ID:C_ID + P]

        x_in = [sem("x_in0"), sem("x_in1")]
        c_in, a_in, cst_in, bout_in, rope_in = sem("c_in"), sem("a_in"), sem("cst_in"), sem("bout_in"), sem("rope_in")
        wmod_in = [sem("wmod_in0"), sem("wmod_in1")]
        grp_in = [sem(f"grp_in{g}") for g in range(GROUPS)]
        out_done = sem("out_done")

        chain = sem("chain")
        bf_ready = sem("bf_ready")
        wsum_ready = sem("wsum_ready")
        silu_exp = sem("silu_exp")
        silu_ready = sem("silu_ready")
        wc_done = sem("wc_done")
        wo_done = sem("wo_done")
        mod_done = sem("mod_done")
        bias_done = sem("bias_done")
        sa_ready = sem("sa_ready")
        wcm_ready = sem("wcm_ready")
        wo_ready = sem("wo_ready")
        gab_ready = sem("gab_ready")
        modb_ready = sem("modb_ready")
        xn_ready = sem("xn_ready")
        xnt_done = sem("xnt_done")
        xnt_ready = sem("xnt_ready")
        c_done = sem("c_done")
        chat_ready = sem("chat_ready")
        cht_done = sem("cht_done")
        cht_ready = sem("cht_ready")
        qkv_done = sem("qkv_done")
        prod_ready = sem("prod_ready")
        v_ready = sem("v_ready")
        sel_done = sem("sel_done")
        qk_hi = sem("qk_hi")
        qk_ready = sem("qk_ready")
        xres_ready = sem("xres_ready")
        s_done = sem("s_done")
        nm_ready = sem("nm_ready")
        e_done = sem("e_done")
        pt_done = sem("pt_done")
        p_hi = sem("p_hi")
        p_lo = sem("p_lo")
        pv_done = sem("pv_done")
        ot_ready = sem("ot_ready")
        ao_done = sem("ao_done")
        x1_ready = sem("x1_ready")
        h_full = sem("h_full")
        h_hi = sem("h_hi")
        h_lo = sem("h_lo")

        dec_done = sem("dec_done")
        wgu_hi, wgu_lo, wd_hi, wd_lo = sem("wgu_hi"), sem("wgu_lo"), sem("wd_hi"), sem("wd_lo")
        gate_done, up_done, down_done = sem("gate_done"), sem("up_done"), sem("down_done")
        gelu_done, inter_done, i_hi, i_lo = sem("gelu_done"), sem("inter_done"), sem("i_hi"), sem("i_lo")
        yt_ready, y_done, y_ready = sem("yt_ready"), sem("y_done"), sem("y_ready")

        x_d = x[0].rearrange("(i p) d -> p i d", p=P)
        out_d = out[0].rearrange("(i p) d -> p i d", p=P)
        wmod_d = wmod.rearrange("(k p) n -> p k n", p=P)

        def bank(b, n=512, p0=0, p1=P):
            return ps[p0:p1, b, 0:n]

        def wgroup(g):
            return wbuf[:, g].rearrange("p e (m n) -> p e m n", m=3)

        def s_at(i):
            return 512 * (S0 + i % 2) if i < HT else 512 * S0

        def pt_at(i):
            return 512 * (PT0 + i % 2) if i < HT else 512 * PT0

        def ot_ps(i):
            return ps[0:2 * DC, GATE if i < HT else PT0, 0:P]

        def ao_ps(i):
            return ps[:, UP if i < HT else PT0 + 1, 0:D]

        block = ctx.enter_context(nc.Block())

        @block.sync
        def _(sp):
            sp.dma_start(xres[:, 0:HT, :], x_d[:, 0:HT, :]).then_inc(x_in[0], 16)
            for h in range(2):
                sp.dma_start(wmod_sb[:, :, 3 * D * h:3 * D * (h + 1)],
                             wmod_d[:, :, 3 * D * h:3 * D * (h + 1)]).then_inc(wmod_in[h], 16)
                if h == 0:
                    sp.dma_start(rope_sb[:], rope).then_inc(rope_in, 16)
                    sp.dma_start(xres[:, HT:, :], x_d[:, HT:, :]).then_inc(x_in[1], 16)
            for g in range(GROUPS):
                sp.dma_start(wbuf[:, g, 0, :].bitcast(I32), packed[g]).then_inc(grp_in[g], 16)
                sp.dma_start(wbuf[:, g, 1, :],
                             scales[g].unsqueeze(1).to_broadcast([P // REP, REP, WORDS])
                             ).then_inc(grp_in[g], 16)
            for h in range(2):
                sp.wait_ge(y_ready, h + 1)
                sp.dma_start(out_d[:, HT * h:HT * (h + 1), :], xres[:, HT * h:HT * (h + 1), :]).then_inc(out_done, 16)
            sp.wait_ge(out_done, 32)

        @block.scalar
        def _(act):
            act.dma_start(c_sb[:], c_col).then_inc(c_in, 16)
            act.dma_start(a64[:], attn64).then_inc(a_in, 16)
            act.dma_start(cst[:], consts).then_inc(cst_in, 16)
            act.dma_start(a32[:], attn32).then_inc(a_in, 16)
            act.dma_start(bout_sb[:], b_out.unsqueeze(0).to_broadcast([P, D])).then_inc(bout_in, 16)

            act.wait_ge(c_in, 16)
            act.activation(silu_t[:, 0, :], c_sb[:], ACT.Exp, scale=-1.0).then_inc(silu_exp, 1)

            def stage_in(h):
                act.wait_ge(xnt_done, 2 * h + 1)
                for ft in range(KT):
                    act.activation(xnT[:, ft, :], bank(S0 + ft), ACT.Copy).then_inc(xnt_ready, 1)
                act.wait_ge(sel_done, h + 1)
                for j in range(2):
                    act.activation(hi_t[:, j, :], bank(PT0 + j), ACT.Copy).then_inc(qk_hi, 1)

            def exps(i):
                act.wait_ge(nm_ready, i + 1)
                if i >= 1:
                    act.wait_ge(pt_done, i)
                n = P * (i + 1)
                act.activation(probs[:, 0:n], flat[:, s_at(i):s_at(i) + n], ACT.Exp, bias=nbias[:, i:i + 1],
                               scale=SCALE, accum_out=den[:, i:i + 1]).then_inc(e_done, 1)

            def probs_hi(i):
                act.wait_ge(pt_done, i + 1)
                if i >= 1:
                    act.wait_ge(pv_done, i)
                n = P * (i + 1)
                act.activation(PS12[:, 0, 0:n], flat[:, pt_at(i):pt_at(i) + n], ACT.Copy).then_inc(p_hi, 1)

            def out_t(i):
                act.wait_ge(pv_done, i + 1)
                if i >= 1:
                    act.wait_ge(ao_done, i)
                act.activation(oT[:], ot_ps(i), ACT.Copy).then_inc(ot_ready, 1)

            def stage_h(h):
                act.wait_ge(xnt_done, 2 * h + 2)
                act.wait_ge(modb_ready, 1)
                if h == 1:
                    act.wait_ge(h_lo, 2)
                for e in range(2):
                    act.activation(hfull[:, e, :], bank(S0 + e), ACT.Identity, bias=mods[:, M_SB + e:M_SB + e + 1],
                                   scale=mods[:, M_CB + e:M_CB + e + 1]).then_inc(h_full, 1)
                for e in range(2):
                    act.wait_ge(h_full, 2 * h + e + 1)
                    act.activation(H[:, h, 0, e, :], hfull[:, e, :], ACT.Copy).then_inc(h_hi, 1)

            def split_gu(G, g, static=True):
                if static and G < GROUPS:
                    act.wait_ge(dec_done, G + 1)
                if not static or G >= 2:
                    act.wait_ge(up_done, 2 * G - 2)
                par = G % 2 if static else g[1]
                src = wgroup(g if static else g[0])
                act.activation(WS[:, par, 0, :, 0:2, :], src[:, :, 0:2, :], ACT.Copy).then_inc(wgu_hi, 1)

            def split_d(G, g, static=True):
                if not static or G >= 2:
                    act.wait_ge(down_done, 2 * G - 2)
                par = G % 2 if static else g[1]
                src = wgroup(g if static else g[0])
                act.activation(WS[:, par, 0, :, 2, :], src[:, :, 2, :], ACT.Copy).then_inc(wd_hi, 1)

            def gelu(n, b, later=True):
                act.wait_ge(gate_done, n + 1)
                if later:
                    act.wait_ge(inter_done, n - 1)
                act.activation(gel[:, b, :], bank(GATE), ACT.Gelu_apprx_tanh).then_inc(gelu_done, 1)

            def inter_hi(n, b, later=True):
                act.wait_ge(inter_done, n + 1)
                if later:
                    act.wait_ge(down_done, n - 1)
                act.activation(IS[:, b, 0, :], inter[:, b, :], ACT.Copy).then_inc(i_hi, 1)

            for h in range(2):
                stage_in(h)
                exps(HT * h)
                for i in range(HT * h, HT * h + HT):
                    probs_hi(i)
                    if i + 1 < HT * h + HT:
                        exps(i + 1)
                    out_t(i)
                stage_h(h)
            split_gu(0, 0)
            split_d(0, 0)
            for n in range(UNITS + 1):
                gelu(n, n % 2, n >= 2)
                inter_hi(n, n % 2, n >= 2)
                G = n // 2 + 1
                if n % 2 == 0:
                    split_gu(G, G % GROUPS)
                else:
                    split_d(G, G % GROUPS)
            with act.Fori(0, 3) as it:
                for j in range(4):
                    n = 4 * it + (UNITS + 1 + j)
                    b = (UNITS + 1 + j) % 2
                    gelu(n, b)
                    inter_hi(n, b)
                    k = 1 + (j + 1) // 2
                    if j % 2 == 0:
                        split_d(2 * it + (GROUPS + k), (2 * it + k, k % 2), static=False)
                    else:
                        split_gu(2 * it + (GROUPS + k), (2 * it + k, k % 2), static=False)
            for n in range(2 * UNITS - 3, 2 * UNITS):
                gelu(n, n % 2)
                inter_hi(n, n % 2)
                if n == 2 * UNITS - 3:
                    split_d(2 * GROUPS - 1, GROUPS - 1)

        @block.gpsimd
        def _(pool):
            pool.wait_ge(cst_in, 16)
            pool.tensor_copy(identb[:], ident).then_inc(bf_ready, 1)
            pool.tensor_copy(maskb[:], cst[:, C_MASK:C_MASK + P]).then_inc(bf_ready, 1)
            pool.wait_ge(a_in, 32)
            pool.tensor_tensor(wsum[:], a64[:, A_KV:A_KV + D], a64[:, A_OUT:A_OUT + D], ALU.add).then_inc(wsum_ready, 1)
            pool.wait_ge(gab_ready, 1)
            for h in range(2):
                pool.wait_ge(xn_ready, 2 * HT * h + HT)
                for j in range(HT):
                    xt = xres[:, HT * h + j, :]
                    last = pool.tensor_tensor(xt, xt, gab[:], ALU.add)
                last.then_inc(xres_ready, 1)

            def low_gu(G, par, g):
                pool.wait_ge(wgu_hi, G + 1)
                pool.tensor_tensor(WS[:, par, 1, :, 0:2, :], wgroup(g)[:, :, 0:2, :],
                                   WS[:, par, 0, :, 0:2, :].bitcast(F32), ALU.subtract).then_inc(wgu_lo, 1)

            def low_d(G, par, g):
                pool.wait_ge(wd_hi, G + 1)
                pool.tensor_tensor(WS[:, par, 1, :, 2, :], wgroup(g)[:, :, 2, :],
                                   WS[:, par, 0, :, 2, :].bitcast(F32), ALU.subtract).then_inc(wd_lo, 1)

            for G in range(GROUPS):
                low_gu(G, G % 2, G)
                low_d(G, G % 2, G)
            with pool.Fori(0, GROUPS // 2) as it:
                for par in range(2):
                    low_gu(2 * it + (GROUPS + par), par, 2 * it + par)
                    low_d(2 * it + (GROUPS + par), par, 2 * it + par)

        @block.vector
        def _(dve):
            steps = [0]

            def link(ins):
                steps[0] += 1
                ins.then_inc(chain, 1)
                dve.wait_ge(chain, steps[0])

            def rsqrt(v, y, t):
                link(dve.tensor_scalar(y.bitcast(I32), v.bitcast(I32), -0.5, RSQRT_SEED, ALU.mult, ALU.add))
                for _ in range(3):
                    link(dve.tensor_tensor(t, y, y, ALU.mult))
                    link(dve.scalar_tensor_tensor(t, t, -0.5, v, ALU.mult, ALU.mult))
                    link(dve.scalar_tensor_tensor(y, t, 1.5, y, ALU.add, ALU.mult))

            def layer_stats(h):
                t0 = HT * h
                for i in range(t0, t0 + HT):
                    dve.bn_stats(stats[:, i, :], xres[:, i, :]).then_inc(chain, 1)
                    steps[0] += 1
                dve.wait_ge(chain, steps[0])
                for i in range(t0, t0 + HT):
                    dve.bn_aggr(mv[:, i, :], stats[:, i, :]).then_inc(chain, 1)
                    steps[0] += 1
                dve.wait_ge(chain, steps[0])
                link(dve.tensor_scalar(rs_v[:], mv[:, t0:t0 + HT, 1], EPS, None, ALU.add))
                rsqrt(rs_v[:], rs_y[:], rs_t[:])

            def norm1(h):
                dve.wait_ge(x_in[h], 16)
                layer_stats(h)
                if h == 1:
                    dve.wait_ge(xnt_done, 2)
                for j in range(HT):
                    i = HT * h + j
                    dve.tensor_scalar(xn[:, j, :], xres[:, i, :], mv[:, i, 0:1], rs_y[:, j:j + 1],
                                      ALU.subtract, ALU.mult).then_inc(xn_ready, 1)

            def norm2(h):
                dve.wait_ge(x1_ready, HT * (h + 1))
                layer_stats(h)
                for j in range(HT):
                    i = HT * h + j
                    dve.tensor_scalar(xn[:, j, :].rearrange("p (e k) -> p e k", e=2),
                                      xres[:, i, :].rearrange("p (k e) -> p e k", e=2),
                                      mv[:, i, 0:1], rs_y[:, j:j + 1],
                                      ALU.subtract, ALU.mult).then_inc(xn_ready, 1)

            def compress(h):
                dve.wait_ge(c_done, h + 1)
                link(dve.tensor_tensor(cc[:], bank(PT0, HT * DC).rearrange("p (j d) -> p j d", j=HT),
                                       cbias[:].unsqueeze(1).to_broadcast([P, HT, DC]), ALU.add))
                link(dve.tensor_tensor(csq[:], cc[:], cc[:], ALU.mult))
                link(dve.tensor_reduce(cvar[:], csq[:], AX_X, ALU.add))
                link(dve.tensor_scalar(cvar[:], cvar[:], 1.0 / DC, EPS, ALU.mult, ALU.add))
                rsqrt(cvar[:], rs_y[:], rs_t[:])
                dve.tensor_tensor(csq[:], cc[:], rs_y[:].unsqueeze(2).to_broadcast([P, HT, DC]),
                                  ALU.mult).then_inc(chat_ready, 1)
                dve.wait_ge(cht_done, h + 1)
                dve.tensor_scalar(chT[:], bank(PT0 + 1, HALF, 0, DC), a32[:, B_GAMMA:B_GAMMA + 1],
                                  a32[:, B_BETA:B_BETA + 1], ALU.mult, ALU.add).then_inc(cht_ready, 1)

            def qkv(h):
                t0 = HALF * h
                dve.wait_ge(qkv_done, h + 1)
                if h == 0:
                    dve.wait_ge(rope_in, 16)
                dve.tensor_tensor(prod[:], bank(S0), rope_sb[:, t0:t0 + HALF], ALU.mult).then_inc(prod_ready, 1)
                v_ps = bank(S0 + 1, HT * DC).rearrange("p (j d) -> p j d", j=HT)
                vt = VS[:, HT * h:HT * (h + 1), :]
                link(dve.tensor_copy(vt[:, :, 0:DC], v_ps))
                dve.tensor_tensor(vt[:, :, DC:], v_ps, vt[:, :, 0:DC].bitcast(F32), ALU.subtract).then_inc(v_ready, 1)
                dst = (QS[:, 0:HALF], KS[:, t0:t0 + HALF])
                dve.wait_ge(sel_done, h + 1)
                for j in range(2):
                    dve.wait_ge(qk_hi, 2 * h + j + 1)
                    dve.scalar_tensor_tensor(dst[j], hi_t[:, j, :].bitcast(F32), cst[:, C_QM + j:C_QM + j + 1],
                                             bank(PT0 + j), ALU.mult, ALU.add).then_inc(qk_ready, 1)

            def row_max(i):
                n = P * (i + 1)
                dve.wait_ge(s_done, i + 1)
                link(dve.tensor_reduce(nmax[:, i:i + 1], flat[:, s_at(i):s_at(i) + n], AX_X, ALU.max, negate=True))
                dve.tensor_scalar(nbias[:, i:i + 1], nmax[:, i:i + 1], SCALE, None, ALU.mult).then_inc(nm_ready, 1)

            def probs_lo(i):
                n = P * (i + 1)
                dve.wait_ge(p_hi, i + 1)
                dve.tensor_tensor(PS12[:, 1, 0:n], flat[:, pt_at(i):pt_at(i) + n], PS12[:, 0, 0:n].bitcast(F32),
                                  ALU.subtract).then_inc(p_lo, 1)
                dve.wait_ge(e_done, i + 1)
                link(dve.reciprocal(rden[:, i:i + 1], den[:, i:i + 1]))

            def residual1(i):
                dve.wait_ge(ao_done, i + 1)
                dve.wait_ge(xres_ready, i // HT + 1)
                dve.scalar_tensor_tensor(xres[:, i, :], ao_ps(i), rden[:, i:i + 1], xres[:, i, :],
                                         ALU.mult, ALU.add).then_inc(x1_ready, 1)

            def h_low(h):
                for e in range(2):
                    dve.wait_ge(h_hi, 2 * h + e + 1)
                    dve.tensor_tensor(H[:, h, 1, e, :], hfull[:, e, :], H[:, h, 0, e, :].bitcast(F32),
                                      ALU.subtract).then_inc(h_lo, 1)

            def decode_bits(g):
                dve.wait_ge(grp_in[g], 32)
                link(dve.tensor_scalar(dec_a[:], wbuf[:, g, 0, :].bitcast(I32), 0xFF, None, ALU.bitwise_and))
                link(dve.tensor_scalar(dec_b[:], dec_a[:], 4097.0, None, ALU.mult))
                link(dve.tensor_scalar(dec_a[:], dec_b[:], 0x70007, 9, ALU.bitwise_and, ALU.logical_shift_left))
                link(dve.tensor_scalar(dec_b[:], dec_b[:], 0x80008, 12, ALU.bitwise_and, ALU.logical_shift_left))
                link(dve.tensor_tensor(dec_v[:], dec_a[:], dec_b[:], ALU.bitwise_or))

            def decode_scale(g):
                vals = dec_v[:].bitcast(F16).rearrange("p (n e) -> p n e", e=2)
                link(dve.scalar_tensor_tensor(wbuf[:, g, 0, :], vals[:, :, 0], FP16_BIAS, wbuf[:, g, 1, :],
                                              ALU.mult, ALU.mult))
                dve.scalar_tensor_tensor(wbuf[:, g, 1, :], vals[:, :, 1], FP16_BIAS, wbuf[:, g, 1, :],
                                         ALU.mult, ALU.mult).then_inc(dec_done, 1)

            def inter_full(n, b, later=True):
                dve.wait_ge(up_done, n + 1)
                dve.wait_ge(gelu_done, n + 1)
                if later:
                    dve.wait_ge(i_hi, n - 1)
                    dve.wait_ge(i_lo, n - 1)
                dve.tensor_tensor(inter[:, b, :], bank(UP), gel[:, b, :], ALU.mult).then_inc(inter_done, 1)

            def inter_low(n, b, later=True):
                dve.wait_ge(i_hi, n + 1)
                if later:
                    dve.wait_ge(down_done, n - 1)
                dve.tensor_tensor(IS[:, b, 1, :], inter[:, b, :], IS[:, b, 0, :].bitcast(F32),
                                  ALU.subtract).then_inc(i_lo, 1)

            def scale_out(h):
                dve.wait_ge(down_done, UNITS * (h + 1))
                if h == 1:
                    dve.wait_ge(y_done, 1)
                for k in range(KT):
                    dve.tensor_scalar(yT[:, k, :], bank(YT + k), mods[:, M_GB + k:M_GB + k + 1], None,
                                      ALU.mult).then_inc(yt_ready, 1)

            def residual2(h):
                dve.wait_ge(y_done, h + 1)
                xt = xres[:, HT * h:HT * (h + 1), :]
                dve.tensor_tensor(xt, flat[:, 512 * S0:512 * S0 + HT * D].rearrange("p (j d) -> p j d", j=HT), xt,
                                  ALU.add).then_inc(y_ready, 1)

            dve.wait_ge(silu_exp, 1)
            link(dve.tensor_scalar(silu_t[:, 1, :], silu_t[:, 0, :], 1.0, None, ALU.add))
            link(dve.reciprocal(silu_t[:, 2, :], silu_t[:, 1, :]))
            dve.tensor_tensor(silu[:], c_sb[:], silu_t[:, 2, :], ALU.mult).then_inc(silu_ready, 1)

            dve.wait_ge(wc_done, 1)
            wc_ps = bank(YT, KT * DC).rearrange("p (k d) -> p k d", k=KT)
            link(dve.tensor_reduce(wc_mean[:], wc_ps, AX_X, ALU.add))
            link(dve.tensor_scalar(wc_mean[:], wc_mean[:], 1.0 / DC, None, ALU.mult))
            link(dve.tensor_tensor(wcc[:], wc_ps, wc_mean[:].unsqueeze(2).to_broadcast([P, KT, DC]), ALU.subtract))

            norm1(0)

            dve.wait_ge(mod_done, 1)
            dve.tensor_copy(mods[:, M_SA:M_SA + KT], bank(GATE)[:, M_SA:M_SA + KT]).then_inc(sa_ready, 1)
            link(dve.tensor_scalar(mods[:, M_CA:M_CA + KT], bank(GATE)[:, M_CA:M_CA + KT], 1.0, None, ALU.add))
            for k in range(KT):
                dve.tensor_scalar(wcm[:, k, :], wcc[:, k, :], mods[:, M_CA + k:M_CA + k + 1], None,
                                  ALU.mult).then_inc(wcm_ready, 1)

            def gate_floor(dst, src, tmp):
                link(dve.tensor_scalar(tmp[:, 0, :], src, 0.0, 2.0, ALU.is_ge, ALU.mult))
                link(dve.tensor_scalar(tmp[:, 0, :], tmp[:, 0, :], -1.0, None, ALU.add))
                link(dve.tensor_tensor(tmp[:, 1, :], src, tmp[:, 0, :], ALU.mult))
                link(dve.scalar_tensor_tensor(dst, tmp[:, 1, :], 0.25, tmp[:, 0, :], ALU.max, ALU.mult))

            gate_floor(ga_b[:], bank(UP, D), ga_t)
            dve.wait_ge(bout_in, 16)
            dve.tensor_tensor(gab[:], ga_b[:], bout_sb[:], ALU.mult).then_inc(gab_ready, 1)
            dve.wait_ge(wo_done, 1)
            dve.tensor_tensor(wo[:], bank(YT + 1, D, 0, 2 * DC), ga_b[0:2 * DC, :], ALU.mult).then_inc(wo_ready, 1)
            dve.wait_ge(bias_done, 1)
            link(dve.tensor_copy(cbias[:], bank(YT)[:, 64:64 + DC]))

            compress(0)
            qkv(0)
            dve.wait_ge(mod_done, 2)
            link(dve.tensor_copy(mods[:, M_SB:M_SB + KT], bank(YT)[:, 128 + M_SB:128 + M_SB + KT]))
            link(dve.tensor_scalar(mods[:, M_CB:M_CB + KT], bank(YT)[:, 128 + M_CB:128 + M_CB + KT], 1.0, None, ALU.add))
            gate_floor(mods[:, M_GB:M_GB + KT], bank(YT)[:, 128 + M_GB:128 + M_GB + KT], gb_t)
            dve.sem_inc(modb_ready, 1)

            for h in range(2):
                if h == 1:
                    norm1(h)
                    compress(h)
                    qkv(h)
                row_max(HT * h)
                for i in range(HT * h, HT * h + HT):
                    if i + 1 < HT * h + HT:
                        row_max(i + 1)
                    probs_lo(i)
                    residual1(i)
                norm2(h)
                h_low(h)
            for g in range(2):
                decode_bits(g)
                decode_scale(g)

            for n in range(UNITS + 1):
                inter_full(n, n % 2, n >= 2)
                inter_low(n, n % 2, n >= 2)
                g = n // 2 + 2
                if g < GROUPS and n % 2 == 0:
                    decode_bits(g)
                elif g < GROUPS:
                    decode_scale(g)
            scale_out(0)
            with dve.Fori(0, 3) as it:
                for j in range(4):
                    n = 4 * it + (UNITS + 1 + j)
                    inter_full(n, (UNITS + 1 + j) % 2)
                    inter_low(n, (UNITS + 1 + j) % 2)
            residual2(0)
            for n in range(2 * UNITS - 3, 2 * UNITS):
                inter_full(n, n % 2)
                inter_low(n, n % 2)
            scale_out(1)
            residual2(1)

        @block.tensor
        def _(pe):
            def mm(o, lhsT, rhs, start=True, stop=True):
                return pe.matmul(o, lhsT, rhs, start=start, stop=stop)

            def products(o, pairs):
                for k, (a, b) in enumerate(pairs):
                    last = mm(o, a, b, k == 0, k == len(pairs) - 1)
                return last

            def mod_columns(o, vec, paired):
                for k in range(KT):
                    base = vec * D + (k if paired else k * P)
                    step = 2 if paired else 1
                    for kt in range(KT):
                        last = mm(o[:, k:k + 1], wmod_sb[:, kt, base:base + step * (P - 1) + 1:step],
                                  silu[:, kt:kt + 1], kt == 0, kt == KT - 1)
                return last

            pe.wait_ge(a_in, 32)
            for k in range(KT):
                last = mm(bank(YT)[:, DC * k:DC * (k + 1)], a64[:, A_KV + P * k:A_KV + P * (k + 1)],
                          a64[:, A_CMP:A_CMP + DC])
            last.then_inc(wc_done, 1)
            pe.wait_ge(wsum_ready, 1)
            mm(bank(YT + 1, D, 0, 2 * DC), a64[:, A_LAT:A_LAT + 2 * DC], wsum[:]).then_inc(wo_done, 1)
            pe.wait_ge(silu_ready, 1)
            pe.wait_ge(wmod_in[0], 16)
            mod_columns(bank(GATE)[:, M_SA:M_SA + KT], SA, False)
            mod_columns(bank(GATE)[:, M_CA:M_CA + KT], CA, False)
            for kt in range(KT):
                last = mm(bank(UP, D), silu[:, kt:kt + 1].to_broadcast([P, P]), wmod_sb[:, kt, GA * D:(GA + 1) * D],
                          kt == 0, kt == KT - 1)
            last.then_inc(mod_done, 1)

            def transpose_tiles(h, norm):
                pe.wait_ge(cst_in, 16)
                for j in range(HT):
                    pe.wait_ge(xn_ready, 2 * HT * h + HT * norm + j + 1)
                    for k in range(KT):
                        last = pe.transpose(flat[:, 512 * (S0 + k) + P * j:512 * (S0 + k) + P * (j + 1)],
                                            xn[:, j, P * k:P * (k + 1)], ident)
                last.then_inc(xnt_done, 1)

            def project(h):
                transpose_tiles(h, 0)
                if h == 0:
                    pe.wait_ge(sa_ready, 1)
                    products(bank(YT)[:, 64:64 + DC], [(mods[:, M_SA + k:M_SA + k + 1].to_broadcast([P, P]), wcc[:, k, :])
                                                       for k in range(KT)]).then_inc(bias_done, 1)
                    pe.wait_ge(wcm_ready, KT)
                pe.wait_ge(xnt_ready, KT * (h + 1))
                if h == 1:
                    pe.wait_ge(x1_ready, HT)
                for j in range(HT):
                    last = products(bank(PT0)[:, DC * j:DC * (j + 1)],
                                    [(xnT[:, k, P * j:P * (j + 1)], wcm[:, k, :]) for k in range(KT)])
                last.then_inc(c_done, 1)
                pe.wait_ge(chat_ready, h + 1)
                for j in range(HT):
                    last = pe.transpose(ps[0:DC, PT0 + 1, P * j:P * (j + 1)], csq[:, j, :], ident)
                last.then_inc(cht_done, 1)
                pe.wait_ge(cht_ready, h + 1)
                mm(bank(S0), a32[:, B_QK:B_QK + 4 * DC], chT[:])
                for j in range(HT):
                    last = mm(bank(S0 + 1)[:, DC * j:DC * (j + 1)], chT[:, P * j:P * (j + 1)], a32[:, B_V:B_V + DC])
                last.then_inc(qkv_done, 1)
                pe.wait_ge(prod_ready, h + 1)
                mm(bank(PT0), cst[:, C_SELQ:C_SELQ + P], prod[:])
                mm(bank(PT0 + 1), cst[:, C_SELK:C_SELK + P], prod[:]).then_inc(sel_done, 1)

            def scores(i):
                h, n = i // HT, P * (i + 1)
                pe.wait_ge(qk_ready, 2 * (h + 1))
                pe.wait_ge(v_ready, h + 1)
                pe.wait_ge(bf_ready, 2)
                if i >= HT + 1 or i in (2, 3):
                    pe.wait_ge(e_done, i - 1 if i < HT else i)
                q = QS[:, P * (i % HT):P * (i % HT + 1)]
                for c0 in range(0, n, 512):
                    c1 = min(n, c0 + 512)
                    at = s_at(i)
                    mm(flat[:, at + c0:at + c1], q, KS[:, c0:c1], True, c1 < n)
                    if c1 == n:
                        mm(flat[:, at + n - P:at + n], identb[:], maskb[:], False, True).then_inc(s_done, 1)

            def transposes(i):
                pe.wait_ge(e_done, i + 1)
                if i >= HT + 1:
                    pe.wait_ge(x1_ready, i)
                elif i in (2, 3):
                    pe.wait_ge(p_lo, i - 1)
                for b in range(i + 1):
                    last = pe.transpose(flat[:, pt_at(i) + P * b:pt_at(i) + P * (b + 1)], probs[:, P * b:P * (b + 1)],
                                        ident)
                last.then_inc(pt_done, 1)

            def attend(i):
                pe.wait_ge(p_hi, i + 1)
                pe.wait_ge(p_lo, i + 1)
                if 1 <= i < HT:
                    pe.wait_ge(ot_ready, i)
                products(ot_ps(i), [(VS[:, b, :], PS12[:, s, P * b:P * (b + 1)])
                                    for s in range(2) for b in range(i + 1)]).then_inc(pv_done, 1)
                pe.wait_ge(ot_ready, i + 1)
                pe.wait_ge(wo_ready, 1)
                if 1 <= i < HT:
                    pe.wait_ge(x1_ready, i)
                mm(ao_ps(i), oT[:], wo[:]).then_inc(ao_done, 1)

            def gate_up(n, G, h, par, e, first=False, later=True):
                if first:
                    pe.wait_ge(h_hi, 2 * (h + 1))
                    pe.wait_ge(h_lo, 2 * (h + 1))
                if e == 0:
                    pe.wait_ge(wgu_hi, G + 1)
                    pe.wait_ge(wgu_lo, G + 1)
                for m, (dst, done) in enumerate(((GATE, gate_done), (UP, up_done))):
                    if later:
                        pe.wait_ge((gelu_done, inter_done)[m], n)
                    products(bank(dst), [(WS[:, par, a, k, m, P * e:P * (e + 1)], H[:, h, b, k, :])
                                         for a, b in ((0, 0), (0, 1), (1, 0)) for k in range(2)]).then_inc(done, 1)

            def down(n, G, h, par, e, first=False, last=False, any_h=None):
                pe.wait_ge(i_hi, n + 1)
                pe.wait_ge(i_lo, n + 1)
                if e == 0:
                    pe.wait_ge(wd_hi, G + 1)
                    pe.wait_ge(wd_lo, G + 1)
                if first and h == 1:
                    pe.wait_ge(yt_ready, KT)
                for k in range(KT):
                    for q, (a, b) in enumerate(((0, 0), (0, 1), (1, 0))):
                        ins = mm(bank(YT + k), WS[:, par, a, e, 2, P * k:P * (k + 1)], IS[:, e, b, :],
                                 first and q == 0, last and q == 2)
                ins.then_inc(down_done, 1)

            def untranspose(h):
                pe.wait_ge(yt_ready, KT * (h + 1))
                for j in range(HT):
                    for k in range(KT):
                        ins = pe.transpose(flat[:, 512 * S0 + D * j + P * k:512 * S0 + D * j + P * (k + 1)],
                                           yT[:, k, P * j:P * (j + 1)], ident)
                ins.then_inc(y_done, 1)

            project(0)
            pe.wait_ge(wmod_in[1], 16)
            pe.wait_ge(chat_ready, 1)
            for m, vec, paired in ((M_SB, SB, True), (M_CB, CB, True), (M_GB, GB, False)):
                last = mod_columns(bank(YT)[:, 128 + m:128 + m + KT], vec, paired)
            last.then_inc(mod_done, 1)
            for h in range(2):
                if h == 1:
                    project(1)
                scores(HT * h)
                for i in range(HT * h, HT * h + HT):
                    if i + 1 < HT * h + HT:
                        scores(i + 1)
                    transposes(i)
                    attend(i)
                transpose_tiles(h, 1)

            gate_up(0, 0, 0, 0, 0, first=True, later=False)
            for n in range(1, UNITS + 1):
                gate_up(n, n // 2, n // UNITS, n // 2 % 2, n % 2, first=(n == UNITS))
                down(n - 1, (n - 1) // 2, 0, (n - 1) // 2 % 2, (n - 1) % 2, first=(n == 1), last=(n == UNITS))
            gate_up(UNITS + 1, GROUPS, 1, 0, 1)
            down(UNITS, GROUPS, 1, 0, 0, first=True)
            gate_up(UNITS + 2, GROUPS + 1, 1, 1, 0)
            down(UNITS + 1, GROUPS, 1, 0, 1)
            untranspose(0)
            with pe.Fori(0, 3) as it:
                for j in range(4):
                    u = 3 + j
                    gate_up(4 * it + (UNITS + u), 2 * it + (GROUPS + u // 2), 1, u // 2 % 2, u % 2)
                    d = u - 1
                    down(4 * it + (UNITS + d), 2 * it + (GROUPS + d // 2), 1, d // 2 % 2, d % 2)
            n = 2 * UNITS - 1
            gate_up(n, n // 2, 1, n // 2 % 2, 1)
            down(n - 1, (n - 1) // 2, 1, (n - 1) // 2 % 2, 0)
            down(n, n // 2, 1, n // 2 % 2, 1, last=True)
            untranspose(1)


def kernel(**inputs):
    import concourse.bacc as bacc
    from concourse.bass_utils import run_bass_kernel_spmd as run

    a = {k: np.asarray(v) for k, v in inputs.items()}
    f32 = np.float32

    consts = np.zeros((P, C_N), f32)
    eye = np.eye(P, dtype=f32)
    consts[:, C_ID:C_ID + P] = eye
    for r in range(4):
        for d in range(DC):
            consts[d, C_SELQ + DC * r + d] = consts[2 * DC + d, C_SELQ + DC * r + d] = 1
            consts[DC + d, C_SELK + DC * r + d] = consts[3 * DC + d, C_SELK + DC * r + d] = 1
    consts[:, C_MASK:C_MASK + P] = np.triu(np.full((P, P), -1e30, f32), 1)
    consts[2 * DC:, C_QM] = -1
    consts[DC:2 * DC, C_KM] = -1
    consts[3 * DC:, C_KM] = -1
    inv_freq = f32(1) / np.power(f32(10000.0), np.arange(0, DC, 2, dtype=f32) / f32(DC))
    angle = (np.arange(T, dtype=f32)[:, None] * inv_freq[None]).T
    cos, sin = np.cos(angle), np.sin(angle)
    rope = np.ascontiguousarray(np.concatenate([cos] * 4 + [-sin, sin] * 2, 0).astype(f32))

    rolled = lambda w: np.concatenate([w[DC // 2:], w[:DC // 2]], 0)
    wq, wkv = a["L0_attn_W_q_comp"], a["L0_attn_W_kv_comp"]
    wk, wv = wkv[:DC], wkv[DC:]
    attn64 = np.ascontiguousarray(np.concatenate([
        a["L0_attn_W_to_kv"], a["L0_attn_W_out_res"].T, a["L0_attn_W_comp2lat"], a["L0_attn_W_comp2lat"],
        a["L0_attn_W_compress"].T], 1))
    attn32 = np.ascontiguousarray(np.concatenate([
        wq.T, wk.T, rolled(wq).T, rolled(wk).T, wv.T, a["L0_attn_ln_gamma"][:, None], a["L0_attn_ln_beta"][:, None]], 1))

    def by_group(w):
        k = w.shape[1]
        return w.reshape(GROUPS, P, 2, k).transpose(0, 3, 2, 1).reshape(GROUPS, k, 2 * P)

    def down_by_group(w):
        return w.T.reshape(GROUPS, -1, D)

    packed = np.ascontiguousarray(np.concatenate([
        by_group(a["L0_ffn_gate_W_packed"]), by_group(a["L0_ffn_up_W_packed"]),
        down_by_group(a["L0_ffn_down_W_packed"])], 2))
    scales = np.ascontiguousarray(np.concatenate([
        by_group(a["L0_ffn_gate_scales"]), by_group(a["L0_ffn_up_scales"]),
        down_by_group(a["L0_ffn_down_scales"])], 2))

    arrays = {
        "x": a["L0_attn_x"], "wmod": a["L0_wmod"],
        "c_col": np.ascontiguousarray(a["L0_c"].reshape(KT, P).T),
        "attn64": attn64, "attn32": attn32, "b_out": a["L0_attn_b_out_res"],
        "consts": consts, "rope": rope, "packed": packed, "scales": scales,
    }
    nc = bacc.Bacc("TRN2", target_bir_lowering=False, num_devices=1)
    ins = {k: np.ascontiguousarray(v) for k, v in arrays.items()}
    args = [nc.dram_tensor(k, v.shape, mybir.dt.from_np(v.dtype), kind="ExternalInput").ap() for k, v in ins.items()]
    out = nc.dram_tensor("out", (1, T, D), F32, kind="ExternalOutput").ap()
    build_block(nc, *args, out)
    return run(nc, [ins], core_ids=[0]).results[0]["out"]
```

```python
from contextlib import ExitStack

import numpy as np

import concourse.bass as bass
from concourse import mybir
from concourse.alu_op_type import AluOpType as ALU

ACT = mybir.ActivationFunctionType
AX_X = mybir.AxisListType.X
F32 = mybir.dt.float32
F32R = mybir.dt.float32r
F16 = mybir.dt.float16
BF16 = mybir.dt.bfloat16
I32 = mybir.dt.int32

P = 128
T, D = 1024, 256
DLAT, DC = 64, 32
FF = 2048
TILES = T // P
HALF = 512
HT = HALF // P
KT = D // P
GROUPS = FF // (2 * P)
UNITS = 2 * GROUPS
WORDS = 3 * 2 * P
BLOCK = 32
REP = BLOCK // 2
EPS = 1e-5
SCALE = float(1.0 / np.sqrt(np.float32(DC)))
RSQRT_SEED = float(0x5F3759DF)
FP16_BIAS = 2.0 ** 14

C_ID, C_SELQ, C_SELK, C_MASK, C_MASKT, C_QM = 0, P, 2 * P, 3 * P, 4 * P, 5 * P
C_KM, C_OM, C_WM, C_N = C_QM + 1, C_QM + 2, C_QM + 3, C_QM + 4
A_KV, A_OUT, A_LAT, A_CMP, A_N = 0, D, 2 * D, 2 * D + 4 * DC, 2 * D + 5 * DC
QK = 3 * DC
OW = D + 2
B_QK, B_V, B_GAMMA, B_BETA, B_N = 0, 4 * DC, 5 * DC, 5 * DC + 1, 5 * DC + 2
SA, CA, GA, SB, CB, GB = range(6)
M_SA, M_CA, M_SB, M_CB, M_GB = 0, 2, 4, 6, 8
RING = 3
N_LN1, N_LNC, N_LN2 = 0, 2, 4
DECODE_STEPS = 7
H1_UNIT = 4


def build_block(nc, x, wmod, c_col, attn64, attn32, b_out, consts, rope, packed, scales, out):
    with ExitStack() as ctx:
        def sb(name, shape, dt=F32):
            return ctx.enter_context(nc.sbuf_tensor(name, shape, dt))

        def sem(name):
            return ctx.enter_context(nc.semaphore(name))

        ps = ctx.enter_context(nc.psum_tensor("ps", [P, 8, 512], F32))
        flat = ps[:].rearrange("p b n -> p (b n)")
        MODA_B, GA_B, WC_B, WO_B = 4, 5, 6, 7
        GATE, UP, YT, OUT = 0, 1, 2, 4

        xres = sb("xres", [P, TILES, D])
        wmod_sb = sb("wmod_sb", [P, KT, 6 * D])
        c_sb = sb("c_sb", [P, KT])
        a64 = sb("a64", [DLAT, A_N])
        a32 = sb("a32", [DC, B_N])
        bout_sb = sb("bout_sb", [P, D])
        cst = sb("cst", [P, C_N])
        rope_sb = sb("rope_sb", [P, T])
        wbuf = sb("wbuf", [P, GROUPS, 2, WORDS])

        identb = sb("identb", [P, P], BF16)
        maskb = sb("maskb", [P, 2, P], BF16)
        silu_t = sb("silu_t", [P, 3, KT])
        silu = sb("silu", [P, KT])
        mods = sb("mods", [P, 10])
        ga_t = sb("ga_t", [P, 2, D])
        ga_b = sb("ga_b", [P, D])
        gab = sb("gab", [P, D])
        gb_t = sb("gb_t", [P, 2, KT])
        wsum = sb("wsum", [DLAT, D])
        wo = sb("wo", [P, D])
        wo_hi = sb("wo_hi", [P, D], F32R)
        WOS = sb("WOS", [P, OW], F32R)
        wc_mean = sb("wc_mean", [P, KT])
        wcc = sb("wcc", [P, KT, DC])
        wcm = sb("wcm", [P, KT, DC])
        cbias = sb("cbias", [P, DC])

        stats = sb("stats", [P, TILES, 6])
        mv = sb("mv", [P, TILES, 2])
        power = sb("power", [P, HT])
        var = sb("var", [P, 6, HT])
        rstd = sb("rstd", [P, 6, HT])
        xn = sb("xn", [P, 2, HT, D])
        xnT = sb("xnT", [P, KT, HALF])
        hfull = xnT
        cc = sb("cc", [P, 2, HT, DC])
        csq = sb("csq", [P, 2, HT, DC])
        chT = sb("chT", [DC, HALF])
        prod = sb("prod", [P, HALF])
        qk_h = sb("qk_h", [P, 2, HALF], F32R)
        QS = sb("QS", [P, 2, HALF], F32R)
        KS = sb("KS", [P, T], F32R)
        VS = sb("VS", [P, TILES, 2, P], F32R)
        nmax_p = sb("nmax_p", [P, HT, 2])
        nmax = sb("nmax", [P, TILES])
        rden = sb("rden", [P, TILES])
        PF = sb("PF", [P, RING, HALF])
        PH = sb("PH", [P, RING, HALF], F32R)
        PL = sb("PL", [P, RING, HALF], F32R)
        o_hi = sb("o_hi", [P, HALF], F32R)
        OS = sb("OS", [P, HALF], F32R)
        H = sb("H", [P, 2, 2, 2, HALF], F32R)

        dec_a = sb("dec_a", [P, WORDS], I32)
        dec_b = sb("dec_b", [P, WORDS], I32)
        WS = sb("WS", [P, 2, 2, 2, 3, 2 * P], F32R)
        wmod_flat = wmod_sb[:].rearrange("p k n -> p (k n)")
        gel = wmod_flat[:, 0:2 * HALF].rearrange("p (b n) -> p b n", b=2)
        inter = wmod_flat[:, 2 * HALF:4 * HALF].rearrange("p (b n) -> p b n", b=2)
        yT = wmod_flat[:, 4 * HALF:6 * HALF].rearrange("p (b n) -> p b n", b=2)
        IS = sb("IS", [P, 2, 2, HALF], F32R)

        ident = cst[:, C_ID:C_ID + P]

        x_in = [sem("x_in0"), sem("x_in1")]
        c_in, a64_in, a32_in, cst_in, bout_in, rope_in = sem("c_in"), sem("a64_in"), sem("a32_in"), sem("cst_in"), sem("bout_in"), sem("rope_in")
        wmod_in = [sem("wmod_in0"), sem("wmod_in1")]
        grp_in = [sem(f"grp_in{g}") for g in range(GROUPS)]
        out_done = sem("out_done")

        chain = sem("chain")
        bf_ready = sem("bf_ready")
        ones_ready = sem("ones_ready")
        wsum_ready = sem("wsum_ready")
        silu_exp = sem("silu_exp")
        silu_ready = sem("silu_ready")
        wc_done = sem("wc_done")
        wo_done = sem("wo_done")
        moda_done = sem("moda_done")
        ga_done = sem("ga_done")
        modb_done = sem("modb_done")
        bias_done = sem("bias_done")
        sa_ready = sem("sa_ready")
        wcm_ready = sem("wcm_ready")
        wo_ready = sem("wo_ready")
        gab_ready = sem("gab_ready")
        modb_ready = sem("modb_ready")
        var_ready = [sem(f"var_ready{k}") for k in range(6)]
        rstd_ready = [sem(f"rstd_ready{k}") for k in range(6)]
        x1n_ready = sem("x1n_ready")
        x2n_ready = sem("x2n_ready")
        t1_done = sem("t1_done")
        t1_ready = sem("t1_ready")
        t2_done = sem("t2_done")
        c_done = sem("c_done")
        chat_ready = sem("chat_ready")
        cht_done = sem("cht_done")
        cht_ready = sem("cht_ready")
        qkv_done = sem("qkv_done")
        prod_ready = sem("prod_ready")
        v_ready = sem("v_ready")
        sel_done = sem("sel_done")
        qk_hi = sem("qk_hi")
        qk_ready = sem("qk_ready")
        xres_ready = sem("xres_ready")
        s_done = sem("s_done")
        s_max = sem("s_max")
        nm_ready = sem("nm_ready")
        m_done = sem("m_done")
        m_ready = sem("m_ready")
        st_done = sem("st_done")
        p_full = sem("p_full")
        p_hi = sem("p_hi")
        p_lo = sem("p_lo")
        pv_done = sem("pv_done")
        o_hi_ready = sem("o_hi_ready")
        o_ready = sem("o_ready")
        ao_done = sem("ao_done")
        x1_ready = sem("x1_ready")
        h_full = sem("h_full")
        h_hi = sem("h_hi")
        h_lo = sem("h_lo")

        dec_done = sem("dec_done")
        wgu_hi, wgu_lo, wd_hi, wd_lo = sem("wgu_hi"), sem("wgu_lo"), sem("wd_hi"), sem("wd_lo")
        gate_done, up_done, down_done = sem("gate_done"), sem("up_done"), sem("down_done")
        gelu_done, inter_done, i_hi, i_lo = sem("gelu_done"), sem("inter_done"), sem("i_hi"), sem("i_lo")
        yt_ready, y_done, y_ready = sem("yt_ready"), sem("y_done"), sem("y_ready")

        x_d = x[0].rearrange("(i p) d -> p i d", p=P)
        out_d = out[0].rearrange("(i p) d -> p i d", p=P)
        wmod_d = wmod.rearrange("(k p) n -> p k n", p=P)

        def bank(b, n=512, p0=0, p1=P):
            return ps[p0:p1, b, 0:n]

        def wgroup(g):
            return wbuf[:, g].rearrange("p e (m n) -> p e m n", m=3)

        def pieces(h):
            return [(j, c0, min(c0 + 512, P * (HT * h + j + 1)))
                    for j in range(HT) for c0 in range(0, P * (HT * h + j + 1), 512)]

        def first_col(h, b):
            return max(0, P * (b - HT * h))

        def blocks(h):
            return [(b, b + HT * h) for b in range(HT * (h + 1))]

        def all_blocks(h):
            return sum(len(blocks(g)) for g in range(h + 1))

        block = ctx.enter_context(nc.Block())

        @block.sync
        def _(sp):
            sp.dma_start(xres[:, 0:HT, :], x_d[:, 0:HT, :]).then_inc(x_in[0], 16)
            sp.dma_start(cst[:], consts).then_inc(cst_in, 16)
            sp.dma_start(wmod_sb[:, :, 0:2 * D], wmod_d[:, :, 0:2 * D]).then_inc(wmod_in[0], 16)
            sp.dma_start(xres[:, HT:, :], x_d[:, HT:, :]).then_inc(x_in[1], 16)
            sp.dma_start(wmod_sb[:, :, 2 * D:], wmod_d[:, :, 2 * D:]).then_inc(wmod_in[1], 16)
            sp.dma_start(rope_sb[:], rope).then_inc(rope_in, 16)
            for g in range(GROUPS):
                sp.dma_start(wbuf[:, g, 0, :].bitcast(I32), packed[g]).then_inc(grp_in[g], 16)
                sp.dma_start(wbuf[:, g, 1, :],
                             scales[g].unsqueeze(1).to_broadcast([P // REP, REP, WORDS])
                             ).then_inc(grp_in[g], 16)
            for h in range(2):
                sp.wait_ge(y_ready, h + 1)
                sp.dma_start(out_d[:, HT * h:HT * (h + 1), :], xres[:, HT * h:HT * (h + 1), :]).then_inc(out_done, 16)
            sp.wait_ge(out_done, 32)

        @block.scalar
        def _(act):
            act.dma_start(c_sb[:], c_col).then_inc(c_in, 16)
            act.dma_start(a64[:], attn64).then_inc(a64_in, 16)
            act.dma_start(a32[:], attn32).then_inc(a32_in, 16)
            act.dma_start(bout_sb[:], b_out.unsqueeze(0).to_broadcast([P, D])).then_inc(bout_in, 16)

            act.wait_ge(c_in, 16)
            act.activation(silu_t[:, 0, :], c_sb[:], ACT.Exp, scale=-1.0).then_inc(silu_exp, 1)

            def norm1_out(h):
                act.wait_ge(t1_done, h + 1)
                if h == 1:
                    act.wait_ge(c_done, 1)
                for k in range(KT):
                    act.activation(xnT[:, k, :], bank(4 * h + k), ACT.Copy).then_inc(t1_ready, 1)

            def qk_high(h):
                act.wait_ge(sel_done, h + 1)
                if h == 1:
                    act.wait_ge(qk_ready, 2)
                for j in range(2):
                    act.activation(qk_h[:, j, :], bank(4 * h + 2 + j), ACT.Copy).then_inc(qk_hi, 1)

            def max_rows(h):
                act.wait_ge(m_done, h + 1)
                act.activation(QS[QK:P, h, :], bank(4 * h + 3, HALF, QK, P), ACT.Copy, scale=1.0 / DC).then_inc(m_ready, 1)

            def exps(h):
                for b, k in blocks(h):
                    c0 = first_col(h, b)
                    act.wait_ge(st_done, k + 1)
                    if k >= RING:
                        act.wait_ge(p_lo, k - RING + 1)
                        act.wait_ge(pv_done, k - RING + 1)
                    src = ps[:, 4 * h + b % 3, c0:HALF]
                    act.activation(PF[:, k % RING, c0:], src, ACT.Exp, scale=SCALE).then_inc(p_full, 1)
                    act.activation(PH[:, k % RING, c0:], src, ACT.Exp, scale=SCALE).then_inc(p_hi, 1)

            def out_high(h):
                act.wait_ge(pv_done, all_blocks(h))
                if h == 1:
                    act.wait_ge(o_ready, 1)
                act.activation(o_hi[:], bank(4 * h + 3), ACT.Copy).then_inc(o_hi_ready, 1)

            def stage_h(h):
                act.wait_ge(t2_done, h + 1)
                act.wait_ge(modb_ready, 1)
                act.wait_ge(c_done, 2)
                if h == 1:
                    act.wait_ge(h_lo, 2)
                for e in range(2):
                    act.activation(hfull[:, e, :], bank(4 * h + e), ACT.Identity, bias=mods[:, M_SB + e:M_SB + e + 1],
                                   scale=mods[:, M_CB + e:M_CB + e + 1]).then_inc(h_full, 1)
                for e in range(2):
                    act.wait_ge(h_full, 2 * h + e + 1)
                    act.activation(H[:, h, 0, e, :], hfull[:, e, :], ACT.Copy).then_inc(h_hi, 1)

            def split_gu(G, g, static=True):
                if static and G < GROUPS:
                    act.wait_ge(dec_done, G + 1)
                if not static or G >= 2:
                    act.wait_ge(up_done, 2 * G - 2)
                par = G % 2 if static else g[1]
                src = wgroup(g if static else g[0])
                act.activation(WS[:, par, 0, :, 0:2, :], src[:, :, 0:2, :], ACT.Copy).then_inc(wgu_hi, 1)

            def split_d(G, g, static=True):
                if not static or G >= 2:
                    act.wait_ge(down_done, 2 * G - 2)
                par = G % 2 if static else g[1]
                src = wgroup(g if static else g[0])
                act.activation(WS[:, par, 0, :, 2, :], src[:, :, 2, :], ACT.Copy).then_inc(wd_hi, 1)

            def gelu(n, b, later=True):
                act.wait_ge(gate_done, n + 1)
                if later:
                    act.wait_ge(inter_done, n - 1)
                act.activation(gel[:, b, :], bank(GATE), ACT.Gelu_apprx_tanh).then_inc(gelu_done, 1)

            def inter_hi(n, b, later=True):
                act.wait_ge(inter_done, n + 1)
                if later:
                    act.wait_ge(down_done, n - 1)
                act.activation(IS[:, b, 0, :], inter[:, b, :], ACT.Copy).then_inc(i_hi, 1)

            norm1_out(0)
            norm1_out(1)
            qk_high(0)
            split_gu(0, 0)
            split_d(0, 0)
            max_rows(0)
            exps(0)
            split_gu(1, 1)
            split_d(1, 1)
            qk_high(1)
            out_high(0)
            stage_h(0)
            max_rows(1)
            exps(1)
            out_high(1)
            for n in range(UNITS + 1):
                gelu(n, n % 2, n >= 2)
                inter_hi(n, n % 2, n >= 2)
                if n == H1_UNIT:
                    stage_h(1)
                G = n // 2 + 1
                if G == 1:
                    continue
                if n % 2 == 0:
                    split_gu(G, G % GROUPS)
                else:
                    split_d(G, G % GROUPS)
            with act.Fori(0, 3) as it:
                for j in range(4):
                    n = 4 * it + (UNITS + 1 + j)
                    b = (UNITS + 1 + j) % 2
                    gelu(n, b)
                    inter_hi(n, b)
                    k = 1 + (j + 1) // 2
                    if j % 2 == 0:
                        split_d(2 * it + (GROUPS + k), (2 * it + k, k % 2), static=False)
                    else:
                        split_gu(2 * it + (GROUPS + k), (2 * it + k, k % 2), static=False)
            for n in range(2 * UNITS - 3, 2 * UNITS):
                gelu(n, n % 2)
                inter_hi(n, n % 2)
                if n == 2 * UNITS - 3:
                    split_d(2 * GROUPS - 1, GROUPS - 1)

        @block.gpsimd
        def _(pool):
            for q, (dst, value) in enumerate(((power[:], -0.5), (KS[QK:P, :].bitcast(F32), 1.0),
                                              (VS[:, :, 0, QK:P].bitcast(F32), 1.0), (VS[:, :, 1, QK:P].bitcast(F32), 0.0),
                                              (WOS[:, D:OW].bitcast(F32), 0.0),
                                              (WOS[QK:P, D:D + 1].bitcast(F32), 2.0 / DC))):
                if q:
                    pool.wait_ge(ones_ready, q)
                pool.memset(dst, value).then_inc(ones_ready, 1)
            pool.wait_ge(ones_ready, 6)

            def rsqrt(k):
                pool.wait_ge(var_ready[k], 1)
                pool.tensor_tensor(rstd[:, k, :], var[:, k, :], power[:], ALU.pow).then_inc(rstd_ready[k], 1)

            def add_bias(h):
                pool.wait_ge(gab_ready, 1)
                pool.wait_ge(x1n_ready, HT * (h + 1))
                for j in range(HT):
                    xt = xres[:, HT * h + j, :]
                    last = pool.tensor_tensor(xt, xt, gab[:], ALU.add)
                last.then_inc(xres_ready, 1)

            pool.wait_ge(a64_in, 16)
            pool.tensor_tensor(wsum[:], a64[:, A_KV:A_KV + D], a64[:, A_OUT:A_OUT + D], ALU.add).then_inc(wsum_ready, 1)
            rsqrt(N_LN1)
            pool.wait_ge(cst_in, 16)
            pool.tensor_copy(identb[:], ident).then_inc(bf_ready, 1)
            pool.tensor_copy(maskb[:].rearrange("p m n -> p (m n)"), cst[:, C_MASK:C_MASK + 2 * P]).then_inc(bf_ready, 1)
            rsqrt(N_LNC)
            rsqrt(N_LN1 + 1)
            add_bias(0)
            rsqrt(N_LNC + 1)
            add_bias(1)
            def low_gu(G, par, g):
                pool.wait_ge(wgu_hi, G + 1)
                pool.tensor_tensor(WS[:, par, 1, :, 0:2, :], wgroup(g)[:, :, 0:2, :],
                                   WS[:, par, 0, :, 0:2, :].bitcast(F32), ALU.subtract).then_inc(wgu_lo, 1)

            def low_d(G, par, g):
                pool.wait_ge(wd_hi, G + 1)
                pool.tensor_tensor(WS[:, par, 1, :, 2, :], wgroup(g)[:, :, 2, :],
                                   WS[:, par, 0, :, 2, :].bitcast(F32), ALU.subtract).then_inc(wd_lo, 1)

            for G in range(GROUPS):
                if G == 2:
                    rsqrt(N_LN2)
                    rsqrt(N_LN2 + 1)
                low_gu(G, G % 2, G)
                low_d(G, G % 2, G)
            with pool.Fori(0, GROUPS // 2) as it:
                for par in range(2):
                    low_gu(2 * it + (GROUPS + par), par, 2 * it + par)
                    low_d(2 * it + (GROUPS + par), par, 2 * it + par)

        @block.vector
        def _(dve):
            steps = [0]

            def link(ins):
                steps[0] += 1
                ins.then_inc(chain, 1)
                dve.wait_ge(chain, steps[0])

            def layer_stats(h, k):
                tiles = range(HT * h, HT * (h + 1))
                for i in tiles:
                    dve.bn_stats(stats[:, i, :], xres[:, i, :]).then_inc(chain, 1)
                    steps[0] += 1
                dve.wait_ge(chain, steps[0])
                for i in tiles:
                    dve.bn_aggr(mv[:, i, :], stats[:, i, :]).then_inc(chain, 1)
                    steps[0] += 1
                dve.wait_ge(chain, steps[0])
                dve.tensor_scalar(var[:, k, :], mv[:, HT * h:HT * (h + 1), 1], EPS, None, ALU.add).then_inc(var_ready[k], 1)

            def stats1(h):
                dve.wait_ge(x_in[h], 16)
                layer_stats(h, N_LN1 + h)

            def norm1(h):
                dve.wait_ge(rstd_ready[N_LN1 + h], 1)
                for j in range(HT):
                    i = HT * h + j
                    dve.tensor_scalar(xn[:, h, j, :], xres[:, i, :], mv[:, i, 0:1], rstd[:, N_LN1 + h, j:j + 1],
                                      ALU.subtract, ALU.mult).then_inc(x1n_ready, 1)

            def stats2(h):
                dve.wait_ge(x1_ready, HT * (h + 1))
                layer_stats(h, N_LN2 + h)

            def norm2(h):
                dve.wait_ge(rstd_ready[N_LN2 + h], 1)
                for j in range(HT):
                    i = HT * h + j
                    dve.tensor_scalar(xn[:, h, j, :].rearrange("p (e k) -> p e k", e=2),
                                      xres[:, i, :].rearrange("p (k e) -> p e k", e=2),
                                      mv[:, i, 0:1], rstd[:, N_LN2 + h, j:j + 1],
                                      ALU.subtract, ALU.mult).then_inc(x2n_ready, 1)

            def compress(h):
                dve.wait_ge(c_done, h + 1)
                link(dve.tensor_tensor(cc[:, h], bank(4 * h + 2, HT * DC).rearrange("p (j d) -> p j d", j=HT),
                                       cbias[:].unsqueeze(1).to_broadcast([P, HT, DC]), ALU.add))
                link(dve.tensor_tensor(csq[:, h], cc[:, h], cc[:, h], ALU.mult))
                link(dve.tensor_reduce(var[:, N_LNC + h, :], csq[:, h], AX_X, ALU.add))
                dve.tensor_scalar(var[:, N_LNC + h, :], var[:, N_LNC + h, :], 1.0 / DC, EPS,
                                  ALU.mult, ALU.add).then_inc(var_ready[N_LNC + h], 1)

            def normc(h):
                dve.wait_ge(rstd_ready[N_LNC + h], 1)
                dve.tensor_tensor(csq[:, h], cc[:, h], rstd[:, N_LNC + h, :].unsqueeze(2).to_broadcast([P, HT, DC]),
                                  ALU.mult).then_inc(chat_ready, 1)

            def gamma_beta(h):
                dve.wait_ge(cht_done, h + 1)
                dve.wait_ge(a32_in, 16)
                if h == 1:
                    dve.wait_ge(qkv_done, 1)
                dve.tensor_scalar(chT[:], bank(4 * h + 3, HALF, 0, DC), a32[:, B_GAMMA:B_GAMMA + 1],
                                  a32[:, B_BETA:B_BETA + 1], ALU.mult, ALU.add).then_inc(cht_ready, 1)

            def rotate(h):
                dve.wait_ge(qkv_done, h + 1)
                dve.wait_ge(rope_in, 16)
                if h == 1:
                    dve.wait_ge(sel_done, 1)
                dve.tensor_tensor(prod[:], bank(4 * h), rope_sb[:, HALF * h:HALF * (h + 1)], ALU.mult).then_inc(prod_ready, 1)

            def split_v(h):
                v_ps = bank(4 * h + 1, HT * DC).rearrange("p (j d) -> p j d", j=HT).unsqueeze(2).to_broadcast([P, HT, 3, DC])
                v_hi, v_lo = [VS[:, HT * h:HT * (h + 1), a, 0:QK].rearrange("p j (r d) -> p j r d", r=3) for a in range(2)]
                link(dve.tensor_copy(v_hi, v_ps))
                dve.tensor_tensor(v_lo, v_ps, v_hi.bitcast(F32), ALU.subtract).then_inc(v_ready, 1)

            def split_qk(h):
                dst = (QS[0:QK, h, :], KS[0:QK, HALF * h:HALF * (h + 1)])
                for j in range(2):
                    dve.wait_ge(qk_hi, 2 * h + j + 1)
                    dve.scalar_tensor_tensor(dst[j], qk_h[0:QK, j, :].bitcast(F32), cst[0:QK, C_QM + j:C_QM + j + 1],
                                             bank(4 * h + 2 + j, HALF, 0, QK), ALU.mult, ALU.add).then_inc(qk_ready, 1)

            def row_max(h, first, last):
                base = len(pieces(0)) * h
                for q in range(first, last):
                    j, c0, c1 = pieces(h)[q]
                    dst = nmax_p[:, j, c0 // 512:c0 // 512 + 1] if h else nmax[:, j:j + 1]
                    dve.wait_ge(s_done, base + q + 1)
                    dve.tensor_reduce(dst, bank(4 * h + q % 3, c1 - c0), AX_X, ALU.max, negate=True).then_inc(s_max, 1)
                if h and last == len(pieces(h)):
                    dve.wait_ge(s_max, base + last)
                    dve.tensor_reduce(nmax[:, HT:], nmax_p[:], AX_X, ALU.min).then_inc(nm_ready, 1)

            def probs_low(h):
                for b, k in blocks(h):
                    c0 = first_col(h, b)
                    dve.wait_ge(p_full, k + 1)
                    dve.wait_ge(p_hi, k + 1)
                    if k >= RING:
                        dve.wait_ge(pv_done, k - RING + 1)
                    dve.tensor_tensor(PL[:, k % RING, c0:], PF[:, k % RING, c0:], PH[:, k % RING, c0:].bitcast(F32),
                                      ALU.subtract).then_inc(p_lo, 1)

            def out_stack(h):
                dve.wait_ge(o_hi_ready, h + 1)
                if h == 1:
                    dve.wait_ge(ao_done, HT)
                dve.scalar_tensor_tensor(OS[:], o_hi[:].bitcast(F32), cst[:, C_OM:C_OM + 1], bank(4 * h + 3),
                                         ALU.mult, ALU.add).then_inc(o_ready, 1)

            def residual1(h):
                dve.wait_ge(xres_ready, h + 1)
                for j in range(HT):
                    i = HT * h + j
                    dve.wait_ge(ao_done, i + 1)
                    link(dve.reciprocal(rden[:, i:i + 1], ps[:, 4 * h + j % 3, D:D + 1]))
                    dve.scalar_tensor_tensor(xres[:, i, :], ps[:, 4 * h + j % 3, 0:D], rden[:, i:i + 1], xres[:, i, :],
                                             ALU.mult, ALU.add).then_inc(x1_ready, 1)

            def h_low(h):
                for e in range(2):
                    dve.wait_ge(h_hi, 2 * h + e + 1)
                    dve.tensor_tensor(H[:, h, 1, e, :], hfull[:, e, :], H[:, h, 0, e, :].bitcast(F32),
                                      ALU.subtract).then_inc(h_lo, 1)

            def decode(g, first=0, last=DECODE_STEPS):
                bits = wbuf[:, g, 0, :].bitcast(I32)
                vals = dec_a[:].bitcast(F16).rearrange("p (n e) -> p n e", e=2)
                if first == 0:
                    dve.wait_ge(grp_in[g], 32)
                    if g:
                        dve.wait_ge(dec_done, g)
                for s in range(first, last):
                    if s:
                        dve.wait_ge(chain, steps[0])
                    steps[0] += s < DECODE_STEPS - 1
                    if s == 0:
                        dve.tensor_scalar(dec_a[:], bits, 0xFF, None, ALU.bitwise_and).then_inc(chain, 1)
                    elif s == 1:
                        dve.tensor_scalar(dec_b[:], dec_a[:], 4097.0, None, ALU.mult).then_inc(chain, 1)
                    elif s == 2:
                        dve.tensor_scalar(dec_a[:], dec_b[:], 0x70007, 9, ALU.bitwise_and,
                                          ALU.logical_shift_left).then_inc(chain, 1)
                    elif s == 3:
                        dve.tensor_scalar(dec_b[:], dec_b[:], 0x80008, 12, ALU.bitwise_and,
                                          ALU.logical_shift_left).then_inc(chain, 1)
                    elif s == 4:
                        dve.tensor_tensor(dec_a[:], dec_a[:], dec_b[:], ALU.bitwise_or).then_inc(chain, 1)
                    elif s == 5:
                        dve.scalar_tensor_tensor(wbuf[:, g, 0, :], vals[:, :, 0], FP16_BIAS, wbuf[:, g, 1, :],
                                                 ALU.mult, ALU.mult).then_inc(chain, 1)
                    else:
                        dve.scalar_tensor_tensor(wbuf[:, g, 1, :], vals[:, :, 1], FP16_BIAS, wbuf[:, g, 1, :],
                                                 ALU.mult, ALU.mult).then_inc(dec_done, 1)

            def inter_full(n, b, later=True):
                dve.wait_ge(up_done, n + 1)
                dve.wait_ge(gelu_done, n + 1)
                if later:
                    dve.wait_ge(i_hi, n - 1)
                    dve.wait_ge(i_lo, n - 1)
                dve.tensor_tensor(inter[:, b, :], bank(UP), gel[:, b, :], ALU.mult).then_inc(inter_done, 1)

            def inter_low(n, b, later=True):
                dve.wait_ge(i_hi, n + 1)
                if later:
                    dve.wait_ge(down_done, n - 1)
                dve.tensor_tensor(IS[:, b, 1, :], inter[:, b, :], IS[:, b, 0, :].bitcast(F32),
                                  ALU.subtract).then_inc(i_lo, 1)

            def scale_out(h):
                dve.wait_ge(down_done, UNITS * (h + 1))
                if h == 1:
                    dve.wait_ge(y_done, 1)
                for k in range(KT):
                    dve.tensor_scalar(yT[:, k, :], bank(YT + k), mods[:, M_GB + k:M_GB + k + 1], None,
                                      ALU.mult).then_inc(yt_ready, 1)

            def residual2(h):
                dve.wait_ge(y_done, h + 1)
                xt = xres[:, HT * h:HT * (h + 1), :]
                dve.tensor_tensor(xt, flat[:, OUT * 512:OUT * 512 + HT * D].rearrange("p (j d) -> p j d", j=HT), xt,
                                  ALU.add).then_inc(y_ready, 1)

            stats1(0)
            dve.wait_ge(silu_exp, 1)
            link(dve.tensor_scalar(silu_t[:, 1, :], silu_t[:, 0, :], 1.0, None, ALU.add))
            link(dve.reciprocal(silu_t[:, 2, :], silu_t[:, 1, :]))
            dve.tensor_tensor(silu[:], c_sb[:], silu_t[:, 2, :], ALU.mult).then_inc(silu_ready, 1)

            dve.wait_ge(wc_done, 1)
            wc_ps = bank(WC_B, KT * DC).rearrange("p (k d) -> p k d", k=KT)
            link(dve.tensor_reduce(wc_mean[:], wc_ps, AX_X, ALU.add))
            link(dve.tensor_scalar(wc_mean[:], wc_mean[:], 1.0 / DC, None, ALU.mult))
            link(dve.tensor_tensor(wcc[:], wc_ps, wc_mean[:].unsqueeze(2).to_broadcast([P, KT, DC]), ALU.subtract))
            norm1(0)
            stats1(1)

            dve.wait_ge(moda_done, 1)
            dve.tensor_copy(mods[:, M_SA:M_SA + KT], bank(MODA_B)[:, M_SA:M_SA + KT]).then_inc(sa_ready, 1)
            link(dve.tensor_scalar(mods[:, M_CA:M_CA + KT], bank(MODA_B)[:, M_CA:M_CA + KT], 1.0, None, ALU.add))
            for k in range(KT):
                dve.tensor_scalar(wcm[:, k, :], wcc[:, k, :], mods[:, M_CA + k:M_CA + k + 1], None,
                                  ALU.mult).then_inc(wcm_ready, 1)

            def gate_floor(dst, src, tmp):
                link(dve.tensor_scalar(tmp[:, 0, :], src, 0.0, 2.0, ALU.is_ge, ALU.mult))
                link(dve.tensor_scalar(tmp[:, 0, :], tmp[:, 0, :], -1.0, None, ALU.add))
                link(dve.tensor_tensor(tmp[:, 1, :], src, tmp[:, 0, :], ALU.mult))
                link(dve.scalar_tensor_tensor(dst, tmp[:, 1, :], 0.25, tmp[:, 0, :], ALU.max, ALU.mult))

            dve.wait_ge(bias_done, 1)
            link(dve.tensor_copy(cbias[:], bank(WC_B)[:, 64:64 + DC]))
            decode(0, 0, 5)
            compress(0)
            norm1(1)
            normc(0)
            dve.wait_ge(ga_done, 1)
            gate_floor(ga_b[:], bank(GA_B, D), ga_t)
            dve.wait_ge(bout_in, 16)
            dve.tensor_tensor(gab[:], ga_b[:], bout_sb[:], ALU.mult).then_inc(gab_ready, 1)
            gamma_beta(0)
            dve.wait_ge(wo_done, 1)
            link(dve.tensor_tensor(wo[:], bank(WO_B, D), ga_b[:], ALU.mult))
            link(dve.tensor_copy(wo_hi[:], wo[:]))
            dve.scalar_tensor_tensor(WOS[:, 0:D], wo_hi[:].bitcast(F32), cst[:, C_WM:C_WM + 1], wo[:],
                                     ALU.mult, ALU.add).then_inc(wo_ready, 1)
            rotate(0)
            split_v(0)
            decode(0, 5)
            decode(1, 0, 5)
            dve.wait_ge(modb_done, 1)
            modb = bank(WO_B)[:, D:D + 10]
            link(dve.tensor_copy(mods[:, M_SB:M_SB + KT], modb[:, M_SB:M_SB + KT]))
            link(dve.tensor_scalar(mods[:, M_CB:M_CB + KT], modb[:, M_CB:M_CB + KT], 1.0, None, ALU.add))
            gate_floor(mods[:, M_GB:M_GB + KT], modb[:, M_GB:M_GB + KT], gb_t)
            dve.sem_inc(modb_ready, 1)
            split_qk(0)
            compress(1)
            row_max(0, 0, HT)
            normc(1)
            gamma_beta(1)
            decode(1, 5)
            rotate(1)
            split_v(1)
            probs_low(0)
            decode(2, 0, 5)
            split_qk(1)
            out_stack(0)
            residual1(0)
            stats2(0)
            row_max(1, 0, 3)
            norm2(0)
            row_max(1, 3, len(pieces(1)))
            h_low(0)
            probs_low(1)
            out_stack(1)
            decode(2, 5)

            for n in range(UNITS + 1):
                g, cut = n // 2 + 3, (0, 1, 4) if n % 2 == 0 else (4, 5, DECODE_STEPS)
                inter_full(n, n % 2, n >= 2)
                if g < GROUPS:
                    decode(g, cut[0], cut[1])
                inter_low(n, n % 2, n >= 2)
                if n == 0:
                    residual1(1)
                elif n == 1:
                    stats2(1)
                elif n == 2:
                    norm2(1)
                elif n == H1_UNIT:
                    h_low(1)
                if g < GROUPS:
                    decode(g, cut[1], cut[2])
            scale_out(0)
            with dve.Fori(0, 3) as it:
                for j in range(4):
                    n = 4 * it + (UNITS + 1 + j)
                    inter_full(n, (UNITS + 1 + j) % 2)
                    inter_low(n, (UNITS + 1 + j) % 2)
            residual2(0)
            for n in range(2 * UNITS - 3, 2 * UNITS):
                inter_full(n, n % 2)
                inter_low(n, n % 2)
            scale_out(1)
            residual2(1)

        @block.tensor
        def _(pe):
            def mm(o, lhsT, rhs, start=True, stop=True):
                return pe.matmul(o, lhsT, rhs, start=start, stop=stop)

            def products(o, pairs):
                for k, (a, b) in enumerate(pairs):
                    last = mm(o, a, b, k == 0, k == len(pairs) - 1)
                return last

            def mod_columns(o, vec, paired):
                for k in range(KT):
                    base = vec * D + (k if paired else k * P)
                    step = 2 if paired else 1
                    for kt in range(KT):
                        last = mm(o[:, k:k + 1], wmod_sb[:, kt, base:base + step * (P - 1) + 1:step],
                                  silu[:, kt:kt + 1], kt == 0, kt == KT - 1)
                return last

            pe.wait_ge(a64_in, 16)
            for k in range(KT):
                last = mm(bank(WC_B)[:, DC * k:DC * (k + 1)], a64[:, A_KV + P * k:A_KV + P * (k + 1)],
                          a64[:, A_CMP:A_CMP + DC])
            last.then_inc(wc_done, 1)
            pe.wait_ge(wsum_ready, 1)
            mm(bank(WO_B, D), a64[:, A_LAT:A_LAT + 4 * DC], wsum[:]).then_inc(wo_done, 1)
            pe.wait_ge(silu_ready, 1)
            pe.wait_ge(wmod_in[0], 16)
            mod_columns(bank(MODA_B)[:, M_SA:M_SA + KT], SA, False)
            mod_columns(bank(MODA_B)[:, M_CA:M_CA + KT], CA, False).then_inc(moda_done, 1)

            def transpose1(h):
                pe.wait_ge(cst_in, 16)
                if h == 1:
                    pe.wait_ge(wcm_ready, KT)
                    pe.wait_ge(gab_ready, 1)
                for j in range(HT):
                    pe.wait_ge(x1n_ready, HT * h + j + 1)
                    for k in range(KT):
                        last = pe.transpose(ps[:, 4 * h + k, P * j:P * (j + 1)], xn[:, h, j, P * k:P * (k + 1)], ident)
                last.then_inc(t1_done, 1)

            def project_c(h):
                pe.wait_ge(wcm_ready, KT)
                pe.wait_ge(t1_ready, KT * (h + 1))
                for j in range(HT):
                    last = products(ps[:, 4 * h + 2, DC * j:DC * (j + 1)],
                                    [(xnT[:, k, P * j:P * (j + 1)], wcm[:, k, :]) for k in range(KT)])
                last.then_inc(c_done, 1)

            def transpose_c(h):
                pe.wait_ge(chat_ready, h + 1)
                if h == 1:
                    pe.wait_ge(modb_ready, 1)
                for j in range(HT):
                    last = pe.transpose(ps[0:DC, 4 * h + 3, P * j:P * (j + 1)], csq[:, h, j, :], ident)
                last.then_inc(cht_done, 1)

            def project_qkv(h):
                pe.wait_ge(cht_ready, h + 1)
                pe.wait_ge(a32_in, 16)
                mm(bank(4 * h), a32[:, B_QK:B_QK + 4 * DC], chT[:])
                for j in range(HT):
                    last = mm(ps[:, 4 * h + 1, DC * j:DC * (j + 1)], chT[:, P * j:P * (j + 1)], a32[:, B_V:B_V + DC])
                last.then_inc(qkv_done, 1)

            def stack_qk(h):
                pe.wait_ge(prod_ready, h + 1)
                mm(bank(4 * h + 2), cst[:, C_SELQ:C_SELQ + P], prod[:])
                mm(bank(4 * h + 3), cst[:, C_SELK:C_SELK + P], prod[:]).then_inc(sel_done, 1)

            def scores(h, first, last):
                pe.wait_ge(qk_ready, 2 * (h + 1))
                pe.wait_ge(bf_ready, 2)
                pe.wait_ge(v_ready, h + 1)
                base = len(pieces(0)) * h
                for q in range(first, last):
                    j, c0, c1 = pieces(h)[q]
                    if q >= 3:
                        pe.wait_ge(s_max, base + q - 2)
                    i = HT * h + j
                    o = bank(4 * h + q % 3, c1 - c0)
                    diag = c1 == P * (i + 1)
                    last = mm(o, QS[0:QK, h, P * j:P * (j + 1)], KS[0:QK, c0:c1], True, not diag)
                    if diag:
                        last = mm(o[:, c1 - c0 - P:], identb[:], maskb[:, 0, :], False, True)
                    last.then_inc(s_done, 1)

            def max_rows(h):
                if h == 0:
                    pe.wait_ge(s_max, len(pieces(0)))
                else:
                    pe.wait_ge(nm_ready, 1)
                for j in range(HT):
                    i = HT * h + j
                    last = mm(ps[QK:P, 4 * h + 3, P * j:P * (j + 1)], nmax[:, i:i + 1].to_broadcast([P, DC]), ident)
                last.then_inc(m_done, 1)

            def key_scores(h, b, k):
                c0 = first_col(h, b)
                pe.wait_ge(m_ready, h + 1)
                pe.wait_ge(ones_ready, 6)
                if b >= 3:
                    pe.wait_ge(p_full, k - 2)
                    pe.wait_ge(p_hi, k - 2)
                diag = b >= HT * h
                last = mm(ps[:, 4 * h + b % 3, c0:HALF], KS[:, P * b:P * (b + 1)], QS[:, h, c0:], True, not diag)
                if diag:
                    last = mm(ps[:, 4 * h + b % 3, c0:c0 + P], identb[:], maskb[:, 1, :], False, True)
                last.then_inc(st_done, 1)

            def attend(h, b, k):
                c0 = first_col(h, b)
                pe.wait_ge(p_hi, k + 1)
                pe.wait_ge(p_lo, k + 1)
                end = len(blocks(h)) - 1
                for q, (v, p) in enumerate(((0, PH), (0, PL), (1, PH))):
                    last = mm(ps[:, 4 * h + 3, c0:HALF], VS[:, b, v, :], p[:, k % RING, c0:], b == 0 and q == 0, b == end and q == 2)
                last.then_inc(pv_done, 1)

            def attention(h):
                todo = blocks(h)
                for q, (b, k) in enumerate(todo):
                    key_scores(h, b, k)
                    if q >= 2:
                        attend(h, *todo[q - 2])
                attend(h, *todo[-2])
                attend(h, *todo[-1])

            def output(h):
                pe.wait_ge(o_ready, h + 1)
                pe.wait_ge(wo_ready, 1)
                for j in range(HT):
                    if j >= 3:
                        pe.wait_ge(x1_ready, HT * h + j - 2)
                    mm(ps[:, 4 * h + j % 3, 0:OW], OS[:, P * j:P * (j + 1)], WOS[:]).then_inc(ao_done, 1)

            def transpose2(h):
                for j in range(HT):
                    pe.wait_ge(x2n_ready, HT * h + j + 1)
                    for k in range(KT):
                        last = pe.transpose(ps[:, 4 * h + k, P * j:P * (j + 1)], xn[:, h, j, P * k:P * (k + 1)], ident)
                last.then_inc(t2_done, 1)

            def gate_up(n, G, h, par, e, first=False, later=True):
                if first:
                    pe.wait_ge(h_hi, 2 * (h + 1))
                    pe.wait_ge(h_lo, 2 * (h + 1))
                if e == 0:
                    pe.wait_ge(wgu_hi, G + 1)
                    pe.wait_ge(wgu_lo, G + 1)
                for m, (dst, done) in enumerate(((GATE, gate_done), (UP, up_done))):
                    if later:
                        pe.wait_ge((gelu_done, inter_done)[m], n)
                    products(bank(dst), [(WS[:, par, a, k, m, P * e:P * (e + 1)], H[:, h, b, k, :])
                                         for a, b in ((0, 0), (0, 1), (1, 0)) for k in range(2)]).then_inc(done, 1)

            def down(n, G, h, par, e, first=False, last=False, any_h=None):
                pe.wait_ge(i_hi, n + 1)
                pe.wait_ge(i_lo, n + 1)
                if e == 0:
                    pe.wait_ge(wd_hi, G + 1)
                    pe.wait_ge(wd_lo, G + 1)
                if first and h == 1:
                    pe.wait_ge(yt_ready, KT)
                for k in range(KT):
                    for q, (a, b) in enumerate(((0, 0), (0, 1), (1, 0))):
                        ins = mm(bank(YT + k), WS[:, par, a, e, 2, P * k:P * (k + 1)], IS[:, e, b, :],
                                 first and q == 0, last and q == 2)
                ins.then_inc(down_done, 1)

            def untranspose(h):
                pe.wait_ge(yt_ready, KT * (h + 1))
                for j in range(HT):
                    for k in range(KT):
                        ins = pe.transpose(flat[:, OUT * 512 + D * j + P * k:OUT * 512 + D * j + P * (k + 1)],
                                           yT[:, k, P * j:P * (j + 1)], ident)
                ins.then_inc(y_done, 1)

            transpose1(0)
            pe.wait_ge(sa_ready, 1)
            products(bank(WC_B)[:, 64:64 + DC], [(mods[:, M_SA + k:M_SA + k + 1].to_broadcast([P, P]), wcc[:, k, :])
                                               for k in range(KT)]).then_inc(bias_done, 1)
            project_c(0)
            pe.wait_ge(wmod_in[1], 16)
            products(bank(GA_B, D), [(silu[:, k:k + 1].to_broadcast([P, P]), wmod_sb[:, k, GA * D:(GA + 1) * D])
                                   for k in range(KT)]).then_inc(ga_done, 1)
            transpose_c(0)
            project_qkv(0)
            transpose1(1)
            stack_qk(0)
            pe.wait_ge(wo_ready, 1)
            for m, vec, paired in ((M_SB, SB, True), (M_CB, CB, True), (M_GB, GB, False)):
                last = mod_columns(bank(WO_B)[:, D + m:D + m + KT], vec, paired)
            last.then_inc(modb_done, 1)
            pe.wait_ge(chat_ready, 1)
            project_c(1)
            scores(0, 0, HT)
            transpose_c(1)
            max_rows(0)
            project_qkv(1)
            attention(0)
            stack_qk(1)
            output(0)
            scores(1, 0, 5)
            transpose2(0)
            scores(1, 5, len(pieces(1)))
            max_rows(1)
            attention(1)

            gate_up(0, 0, 0, 0, 0, first=True, later=False)
            for n in range(1, UNITS + 1):
                gate_up(n, n // 2, n // UNITS, n // 2 % 2, n % 2, first=(n == UNITS))
                if n == 1:
                    output(1)
                elif n == H1_UNIT:
                    transpose2(1)
                down(n - 1, (n - 1) // 2, 0, (n - 1) // 2 % 2, (n - 1) % 2, first=(n == 1), last=(n == UNITS))
            gate_up(UNITS + 1, GROUPS, 1, 0, 1)
            down(UNITS, GROUPS, 1, 0, 0, first=True)
            gate_up(UNITS + 2, GROUPS + 1, 1, 1, 0)
            down(UNITS + 1, GROUPS, 1, 0, 1)
            untranspose(0)
            with pe.Fori(0, 3) as it:
                for j in range(4):
                    u = 3 + j
                    gate_up(4 * it + (UNITS + u), 2 * it + (GROUPS + u // 2), 1, u // 2 % 2, u % 2)
                    d = u - 1
                    down(4 * it + (UNITS + d), 2 * it + (GROUPS + d // 2), 1, d // 2 % 2, d % 2)
            n = 2 * UNITS - 1
            gate_up(n, n // 2, 1, n // 2 % 2, 1)
            down(n - 1, (n - 1) // 2, 1, (n - 1) // 2 % 2, 0)
            down(n, n // 2, 1, n // 2 % 2, 1, last=True)
            untranspose(1)


def kernel(**inputs):
    import concourse.bacc as bacc
    from concourse.bass_utils import run_bass_kernel_spmd as run

    a = {k: np.asarray(v) for k, v in inputs.items()}
    f32 = np.float32

    consts = np.zeros((P, C_N), f32)
    eye = np.eye(P, dtype=f32)
    consts[:, C_ID:C_ID + P] = eye
    for r in range(3):
        for d in range(DC):
            consts[d, C_SELQ + DC * r + d] = consts[2 * DC + d, C_SELQ + DC * r + d] = 1
            consts[DC + d, C_SELK + DC * r + d] = consts[3 * DC + d, C_SELK + DC * r + d] = 1
    consts[:, C_MASK:C_MASK + P] = np.triu(np.full((P, P), -1e30, f32), 1)
    consts[:, C_MASKT:C_MASKT + P] = np.tril(np.full((P, P), -1e30, f32), -1)
    consts[2 * DC:QK, C_QM] = -1
    consts[DC:2 * DC, C_KM] = -1
    consts[DC:2 * DC, C_OM] = -1
    consts[QK + DC // 2:, C_OM] = -1
    consts[2 * DC:QK, C_WM] = -1
    inv_freq = f32(1) / np.power(f32(10000.0), np.arange(0, DC, 2, dtype=f32) / f32(DC))
    angle = (np.arange(T, dtype=f32)[:, None] * inv_freq[None]).T
    cos, sin = np.cos(angle), np.sin(angle)
    rope = np.ascontiguousarray(np.concatenate([cos] * 4 + [-sin, sin] * 2, 0).astype(f32))

    rolled = lambda w: np.concatenate([w[DC // 2:], w[:DC // 2]], 0)
    wq, wkv = a["L0_attn_W_q_comp"], a["L0_attn_W_kv_comp"]
    wk, wv = wkv[:DC], wkv[DC:]
    attn64 = np.ascontiguousarray(np.concatenate([
        a["L0_attn_W_to_kv"], a["L0_attn_W_out_res"].T] + [a["L0_attn_W_comp2lat"]] * 3 + [
        np.zeros((DLAT, DC), f32), a["L0_attn_W_compress"].T], 1))
    attn32 = np.ascontiguousarray(np.concatenate([
        wq.T, wk.T, rolled(wq).T, rolled(wk).T, wv.T, a["L0_attn_ln_gamma"][:, None], a["L0_attn_ln_beta"][:, None]], 1))

    def by_group(w):
        k = w.shape[1]
        return w.reshape(GROUPS, P, 2, k).transpose(0, 3, 2, 1).reshape(GROUPS, k, 2 * P)

    def down_by_group(w):
        return w.T.reshape(GROUPS, -1, D)

    packed = np.ascontiguousarray(np.concatenate([
        by_group(a["L0_ffn_gate_W_packed"]), by_group(a["L0_ffn_up_W_packed"]),
        down_by_group(a["L0_ffn_down_W_packed"])], 2))
    scales = np.ascontiguousarray(np.concatenate([
        by_group(a["L0_ffn_gate_scales"]), by_group(a["L0_ffn_up_scales"]),
        down_by_group(a["L0_ffn_down_scales"])], 2))

    arrays = {
        "x": a["L0_attn_x"], "wmod": a["L0_wmod"],
        "c_col": np.ascontiguousarray(a["L0_c"].reshape(KT, P).T),
        "attn64": attn64, "attn32": attn32, "b_out": a["L0_attn_b_out_res"],
        "consts": consts, "rope": rope, "packed": packed, "scales": scales,
    }
    nc = bacc.Bacc("TRN2", target_bir_lowering=False, num_devices=1)
    ins = {k: np.ascontiguousarray(v) for k, v in arrays.items()}
    args = [nc.dram_tensor(k, v.shape, mybir.dt.from_np(v.dtype), kind="ExternalInput").ap() for k, v in ins.items()]
    out = nc.dram_tensor("out", (1, T, D), F32, kind="ExternalOutput").ap()
    build_block(nc, *args, out)
    return run(nc, [ins], core_ids=[0]).results[0]["out"]
```

```python
from contextlib import ExitStack

import numpy as np

import concourse.bass as bass
from concourse import mybir
from concourse.alu_op_type import AluOpType as ALU

ACT = mybir.ActivationFunctionType
AX_X = mybir.AxisListType.X
F32 = mybir.dt.float32
F32R = mybir.dt.float32r
F16 = mybir.dt.float16
BF16 = mybir.dt.bfloat16
I32 = mybir.dt.int32

P = 128
T, D = 1024, 256
DLAT, DC = 64, 32
FF = 2048
TILES = T // P
HALF = 512
HT = HALF // P
KT = D // P
GROUPS = FF // (2 * P)
UNITS = 2 * GROUPS
WORDS = 3 * 2 * P
BLOCK = 32
REP = BLOCK // 2
EPS = 1e-5
SCALE = float(1.0 / np.sqrt(np.float32(DC)))
RSQRT_SEED = float(0x5F3759DF)
FP16_BIAS = 2.0 ** 14

C_ID, C_SELQ, C_SELK, C_MASK, C_MASKT, C_QM = 0, P, 2 * P, 3 * P, 4 * P, 5 * P
C_KM, C_OM, C_WM, C_N = C_QM + 1, C_QM + 2, C_QM + 3, C_QM + 4
A_KV, A_OUT, A_LAT, A_CMP, A_N = 0, D, 2 * D, 2 * D + 4 * DC, 2 * D + 5 * DC
QK = 3 * DC
OW = D + 2
B_QK, B_V, B_GAMMA, B_BETA, B_N = 0, 4 * DC, 5 * DC, 5 * DC + 1, 5 * DC + 2
SA, CA, GA, SB, CB, GB = range(6)
M_SA, M_CA, M_SB, M_CB, M_N = 0, 2, 4, 6, 8
RING = 3
N_LN1, N_LNC, N_LN2 = 0, 2, 4
DECODE_STEPS = 7
EARLY = 2
POOL_UNITS = 2 * (GROUPS - 1)
STEPS_AT_START = 8
H0_BLOCK = 4
H1_UNIT = 12


def build_block(nc, x, wmod, c_col, attn64, attn32, b_out, consts, rope, packed, scales, out):
    with ExitStack() as ctx:
        def sb(name, shape, dt=F32):
            return ctx.enter_context(nc.sbuf_tensor(name, shape, dt))

        def sem(name):
            return ctx.enter_context(nc.semaphore(name))

        ps = ctx.enter_context(nc.psum_tensor("ps", [P, 8, 512], F32))
        MODA_B, GA_B, WC_B, WO_B = 4, 5, 6, 7
        GATE, UP, Y = 0, 1, 2

        xres = sb("xres", [P, TILES, D])
        wmod_sb = sb("wmod_sb", [P, KT, 6 * D])
        c_sb = sb("c_sb", [P, KT])
        a64 = sb("a64", [DLAT, A_N])
        a32 = sb("a32", [DC, B_N])
        bout_sb = sb("bout_sb", [P, D])
        cst = sb("cst", [P, C_N])
        rope_sb = sb("rope_sb", [P, T])
        wbuf = sb("wbuf", [P, GROUPS, 2, WORDS])

        identb = sb("identb", [P, P], BF16)
        maskb = sb("maskb", [P, 2, P], BF16)
        idle = sb("idle", [P, 512], BF16)
        silu_t = sb("silu_t", [P, 3, KT])
        silu = sb("silu", [P, KT])
        mods = sb("mods", [P, M_N])
        ga_t = sb("ga_t", [P, 2, D])
        ga_b = sb("ga_b", [P, D])
        gab = sb("gab", [P, D])
        gb_b = sb("gb_b", [P, D])
        wsum = sb("wsum", [DLAT, D])
        wo = sb("wo", [P, D])
        wo_hi = sb("wo_hi", [P, D], F32R)
        WOS = sb("WOS", [P, OW], F32R)
        wc_mean = sb("wc_mean", [P, KT])
        wcc = sb("wcc", [P, KT, DC])
        wcm = sb("wcm", [P, KT, DC])
        cbias = sb("cbias", [P, DC])

        stats = sb("stats", [P, TILES, 6])
        mv = sb("mv", [P, TILES, 2])
        power = sb("power", [P, HT])
        var = sb("var", [P, 6, HT])
        rstd = sb("rstd", [P, 6, HT])
        xn = sb("xn", [P, 2, HT, D])
        xnT = sb("xnT", [P, KT, HALF])
        hfull = xnT
        cc = sb("cc", [P, 2, HT, DC])
        csq = sb("csq", [P, 2, HT, DC])
        chT = sb("chT", [DC, HALF])
        prod = sb("prod", [P, HALF])
        qk_h = sb("qk_h", [P, 2, HALF], F32R)
        QS = sb("QS", [P, 2, HALF], F32R)
        KS = sb("KS", [P, T], F32R)
        VS = sb("VS", [P, TILES, 2, P], F32R)
        nmax_p = sb("nmax_p", [P, HT, 2])
        nmax = sb("nmax", [P, TILES])
        rden = sb("rden", [P, TILES])
        PF = sb("PF", [P, RING, HALF])
        PH = sb("PH", [P, RING, HALF], F32R)
        PL = sb("PL", [P, RING, HALF], F32R)
        o_hi = sb("o_hi", [P, HALF], F32R)
        OS = sb("OS", [P, HALF], F32R)
        H = sb("H", [P, 2, 2, 2, HALF], F32R)

        dec_a = sb("dec_a", [P, WORDS], I32)
        dec_b = sb("dec_b", [P, WORDS], I32)
        WS = sb("WS", [P, 2, 2, 2, 3, 2 * P], F32R)
        wmod_flat = wmod_sb[:].rearrange("p k n -> p (k n)")
        gel = wmod_flat[:, 0:2 * HALF].rearrange("p (b n) -> p b n", b=2)
        inter = wmod_flat[:, 2 * HALF:4 * HALF].rearrange("p (b n) -> p b n", b=2)
        ys = wmod_flat[:, 4 * HALF:6 * HALF].rearrange("p (j d) -> p j d", j=HT)
        IS = sb("IS", [P, 2, 2, HALF], F32R)

        ident = cst[:, C_ID:C_ID + P]

        x_in = [sem("x_in0"), sem("x_in1")]
        c_in, a64_in, a32_in, cst_in, bout_in, rope_in = sem("c_in"), sem("a64_in"), sem("a32_in"), sem("cst_in"), sem("bout_in"), sem("rope_in")
        wmod_in = [sem("wmod_in0"), sem("wmod_in1")]
        grp_in = [sem(f"grp_in{g}") for g in range(GROUPS)]
        out_done = sem("out_done")

        chain = sem("chain")
        idle_ready = sem("idle_ready")
        bf_ready = sem("bf_ready")
        ones_ready = sem("ones_ready")
        wsum_ready = sem("wsum_ready")
        silu_exp = sem("silu_exp")
        silu_ready = sem("silu_ready")
        wc_done = sem("wc_done")
        wo_done = sem("wo_done")
        moda_done = sem("moda_done")
        ga_done = sem("ga_done")
        modb_done = sem("modb_done")
        gb_done = sem("gb_done")
        gb_out = sem("gb_out")
        bias_done = sem("bias_done")
        sa_ready = sem("sa_ready")
        wcm_ready = sem("wcm_ready")
        wo_ready = sem("wo_ready")
        gab_ready = sem("gab_ready")
        modb_ready = sem("modb_ready")
        var_ready = [sem(f"var_ready{k}") for k in range(6)]
        rstd_ready = [sem(f"rstd_ready{k}") for k in range(6)]
        x1n_ready = sem("x1n_ready")
        x2n_ready = sem("x2n_ready")
        t1_done = sem("t1_done")
        t1_ready = sem("t1_ready")
        t2_done = sem("t2_done")
        c_done = sem("c_done")
        chat_ready = sem("chat_ready")
        cht_done = sem("cht_done")
        cht_ready = sem("cht_ready")
        qk_done = sem("qk_done")
        qkv_done = sem("qkv_done")
        prod_ready = sem("prod_ready")
        v_hi_ready = sem("v_hi_ready")
        v_ready = sem("v_ready")
        sel_done = sem("sel_done")
        qk_hi = sem("qk_hi")
        qk_ready = sem("qk_ready")
        xres_ready = sem("xres_ready")
        s_done = sem("s_done")
        s_max = sem("s_max")
        nm_ready = sem("nm_ready")
        m_done = sem("m_done")
        m_ready = sem("m_ready")
        st_done = sem("st_done")
        p_full = sem("p_full")
        p_hi = sem("p_hi")
        p_lo = [sem("p_lo"), sem("p_lo_pool")]
        pv_done = sem("pv_done")
        o_hi_ready = sem("o_hi_ready")
        o_ready = sem("o_ready")
        ao_done = sem("ao_done")
        x1_ready = sem("x1_ready")
        h_full = sem("h_full")
        h_hi = sem("h_hi")
        h_lo = sem("h_lo")

        dec_done = sem("dec_done")
        wgu_hi, wgu_lo, wd_hi, wd_lo = sem("wgu_hi"), sem("wgu_lo"), sem("wd_hi"), sem("wd_lo")
        gate_done, up_done, down_done = sem("gate_done"), sem("up_done"), sem("down_done")
        gelu_done, inter_done, i_hi, i_lo = sem("gelu_done"), sem("inter_done"), sem("i_hi"), sem("i_lo")
        half_done = sem("half_done")
        ys_ready, y_ready = sem("ys_ready"), sem("y_ready")

        x_d = x[0].rearrange("(i p) d -> p i d", p=P)
        out_d = out[0].rearrange("(i p) d -> p i d", p=P)
        wmod_d = wmod.rearrange("(k p) n -> p k n", p=P)

        def bank(b, n=512, p0=0, p1=P):
            return ps[p0:p1, b, 0:n]

        def wgroup(g):
            return wbuf[:, g].rearrange("p e (m n) -> p e m n", m=3)

        def pieces(h):
            return [(j, c0, min(c0 + 512, P * (HT * h + j + 1)))
                    for j in range(HT) for c0 in range(0, P * (HT * h + j + 1), 512)]

        def low_maker(k):
            pool = k >= HT and k % 2
            return p_lo[pool], len([j for j in range(k + 1) if (j >= HT and j % 2) == pool])

        def probs_low(engine, h, first, last):
            for b, k in blocks(h)[first:last]:
                c0 = first_col(h, b)
                engine.wait_ge(p_full, k + 1)
                engine.wait_ge(p_hi, k + 1)
                if k >= RING:
                    engine.wait_ge(pv_done, k - RING + 1)
                engine.tensor_tensor(PL[:, k % RING, c0:], PF[:, k % RING, c0:], PH[:, k % RING, c0:].bitcast(F32),
                                     ALU.subtract).then_inc(low_maker(k)[0], 1)

        def first_col(h, b):
            return max(0, P * (b - HT * h))

        def blocks(h):
            return [(b, b + HT * h) for b in range(HT * (h + 1))]

        def all_blocks(h):
            return sum(len(blocks(g)) for g in range(h + 1))

        def v_views(h):
            v_ps = bank(4 * h + 1, HT * DC).rearrange("p (j d) -> p j d", j=HT).unsqueeze(2).to_broadcast([P, HT, 3, DC])
            return v_ps, [VS[:, HT * h:HT * (h + 1), a, 0:QK].rearrange("p j (r d) -> p j r d", r=3) for a in range(2)]

        def inter_low(engine, n, b, later=True):
            engine.wait_ge(inter_done, n + 1)
            engine.wait_ge(i_hi, n + 1)
            if later:
                engine.wait_ge(down_done, n - 1)
            engine.tensor_tensor(IS[:, b, 1, :], inter[:, b, :], IS[:, b, 0, :].bitcast(F32),
                                 ALU.subtract).then_inc(i_lo, 1)

        def unit_banks(n):
            return (Y, Y + 1) if isinstance(n, int) and n == 1 else (GATE, UP)

        block = ctx.enter_context(nc.Block())

        @block.sync
        def _(sp):
            sp.dma_start(xres[:, 0:HT, :], x_d[:, 0:HT, :]).then_inc(x_in[0], 16)
            sp.dma_start(cst[:], consts).then_inc(cst_in, 16)
            sp.dma_start(wmod_sb[:, :, 0:2 * D], wmod_d[:, :, 0:2 * D]).then_inc(wmod_in[0], 16)
            sp.dma_start(xres[:, HT:, :], x_d[:, HT:, :]).then_inc(x_in[1], 16)
            sp.dma_start(wmod_sb[:, :, 2 * D:], wmod_d[:, :, 2 * D:]).then_inc(wmod_in[1], 16)
            sp.dma_start(rope_sb[:], rope).then_inc(rope_in, 16)
            for g in range(GROUPS):
                sp.dma_start(wbuf[:, g, 0, :].bitcast(I32), packed[g]).then_inc(grp_in[g], 16)
                sp.dma_start(wbuf[:, g, 1, :],
                             scales[g].unsqueeze(1).to_broadcast([P // REP, REP, WORDS])
                             ).then_inc(grp_in[g], 16)
            for i in range(0, TILES, 2):
                sp.wait_ge(y_ready, i + 2)
                sp.dma_start(out_d[:, i:i + 2, :], xres[:, i:i + 2, :]).then_inc(out_done, 16)
            sp.wait_ge(out_done, 16 * TILES // 2)

        @block.scalar
        def _(act):
            act.dma_start(c_sb[:], c_col).then_inc(c_in, 16)
            act.dma_start(a64[:], attn64).then_inc(a64_in, 16)
            act.dma_start(a32[:], attn32).then_inc(a32_in, 16)
            act.dma_start(bout_sb[:], b_out.unsqueeze(0).to_broadcast([P, D])).then_inc(bout_in, 16)

            act.wait_ge(c_in, 16)
            act.activation(silu_t[:, 0, :], c_sb[:], ACT.Exp, scale=-1.0).then_inc(silu_exp, 1)

            def norm1_out(h):
                act.wait_ge(t1_done, h + 1)
                if h == 1:
                    act.wait_ge(c_done, 1)
                for k in range(KT) if h else (0,):
                    act.activation(xnT[:, k, :], bank(4 * h + k), ACT.Copy).then_inc(t1_ready, 1)

            def qk_high(h):
                act.wait_ge(sel_done, h + 1)
                if h == 1:
                    act.wait_ge(qk_ready, 2)
                for j in range(2):
                    act.activation(qk_h[:, j, :], bank(4 * h + 2 + j), ACT.Copy).then_inc(qk_hi, 1)

            def v_high(h):
                act.wait_ge(qkv_done, h + 1)
                v_ps, (v_hi, _) = v_views(h)
                act.activation(v_hi, v_ps, ACT.Copy).then_inc(v_hi_ready, 1)

            def max_rows(h):
                act.wait_ge(m_done, h + 1)
                act.activation(QS[QK:P, h, :], bank(4 * h + 3, HALF, QK, P), ACT.Copy, scale=1.0 / DC).then_inc(m_ready, 1)

            def exps(h, first, last):
                for b, k in blocks(h)[first:last]:
                    c0 = first_col(h, b)
                    act.wait_ge(st_done, k + 1)
                    if k >= RING:
                        act.wait_ge(*low_maker(k - RING))
                        act.wait_ge(pv_done, k - RING + 1)
                    src = ps[:, 4 * h + b % 3, c0:HALF]
                    act.activation(PF[:, k % RING, c0:], src, ACT.Exp, scale=SCALE).then_inc(p_full, 1)
                    act.activation(PH[:, k % RING, c0:], src, ACT.Exp, scale=SCALE).then_inc(p_hi, 1)

            def out_high(h):
                act.wait_ge(pv_done, all_blocks(h))
                if h == 1:
                    act.wait_ge(o_ready, 1)
                act.activation(o_hi[:], bank(4 * h + 3), ACT.Copy).then_inc(o_hi_ready, 1)

            def stage_h0():
                act.wait_ge(t2_done, 1)
                act.wait_ge(modb_ready, 2)
                for e in range(2):
                    if e == 1:
                        act.wait_ge(h_full, 1)
                    act.activation(H[:, 0, 0, e, :], bank(e), ACT.Identity, bias=mods[:, M_SB + e:M_SB + e + 1],
                                   scale=mods[:, M_CB + e:M_CB + e + 1]).then_inc(h_hi, 1)

            def stage_h1(e):
                act.wait_ge(t2_done, 2)
                act.wait_ge(h_lo, 2)
                act.activation(hfull[:, e, :], bank(4 + e), ACT.Identity, bias=mods[:, M_SB + e:M_SB + e + 1],
                               scale=mods[:, M_CB + e:M_CB + e + 1]).then_inc(h_full, 1)
                act.wait_ge(h_full, 2 + e + 1)
                act.activation(H[:, 1, 0, e, :], hfull[:, e, :], ACT.Copy).then_inc(h_hi, 1)

            def split_gu(G, g, static=True):
                if static and G < GROUPS:
                    act.wait_ge(dec_done, G + 1)
                if not static or G >= 2:
                    act.wait_ge(up_done, 2 * G - 2)
                par = G % 2 if static else g[1]
                src = wgroup(g if static else g[0])
                act.activation(WS[:, par, 0, :, 0:2, :], src[:, :, 0:2, :], ACT.Copy).then_inc(wgu_hi, 1)

            def split_d(G, g, static=True):
                if not static or G >= 2:
                    act.wait_ge(down_done, 2 * G - 2)
                par = G % 2 if static else g[1]
                src = wgroup(g if static else g[0])
                act.activation(WS[:, par, 0, :, 2, :], src[:, :, 2, :], ACT.Copy).then_inc(wd_hi, 1)

            def gelu(n, b, later=True):
                act.wait_ge(gate_done, n + 1)
                if later:
                    act.wait_ge(inter_done, n - 1)
                act.activation(gel[:, b, :], bank(unit_banks(n)[0]), ACT.Gelu_apprx_tanh).then_inc(gelu_done, 1)

            def inter_hi(n, b, later=True):
                act.wait_ge(inter_done, n + 1)
                if later:
                    act.wait_ge(down_done, n - 1)
                act.activation(IS[:, b, 0, :], inter[:, b, :], ACT.Copy).then_inc(i_hi, 1)

            norm1_out(0)
            v_high(0)
            qk_high(0)
            norm1_out(1)
            max_rows(0)
            exps(0, 0, HT)
            out_high(0)
            v_high(1)
            split_gu(0, 0)
            split_d(0, 0)
            qk_high(1)
            act.wait_ge(gb_done, 1)
            act.activation(gb_b[:], bank(3, D), ACT.Copy).then_inc(gb_out, 1)
            max_rows(1)
            exps(1, 0, H0_BLOCK)
            stage_h0()
            exps(1, H0_BLOCK, 2 * HT - 1)
            split_gu(1, 1)
            exps(1, 2 * HT - 1, 2 * HT)
            split_d(1, 1)
            for n in range(UNITS + 2):
                G = n // 2 + 1
                if n % 2 == 0 and G > 1:
                    split_gu(G, G % GROUPS)
                gelu(n, n % 2, n >= 2)
                if n == 0:
                    out_high(1)
                inter_hi(n, n % 2, n >= 2)
                if n % 2 and G > 1:
                    split_d(G, G % GROUPS)
                if n in (H1_UNIT, H1_UNIT + 1):
                    stage_h1(n - H1_UNIT)
            with act.Fori(0, 3) as it:
                for j in range(4):
                    k = 2 + j // 2
                    if j % 2 == 0:
                        split_gu(2 * it + (GROUPS + k), (2 * it + k, k % 2), static=False)
                    n = 4 * it + (UNITS + 2 + j)
                    gelu(n, j % 2)
                    inter_hi(n, j % 2)
                    if j % 2:
                        split_d(2 * it + (GROUPS + k), (2 * it + k, k % 2), static=False)
            for n in range(2 * UNITS - 2, 2 * UNITS):
                gelu(n, n % 2)
                inter_hi(n, n % 2)

        @block.gpsimd
        def _(pool):
            pool.memset(idle[:], 0.0).then_inc(idle_ready, 1)
            for q, (dst, value) in enumerate(((power[:], -0.5), (KS[QK:P, :].bitcast(F32), 1.0),
                                              (VS[:, :, 0, QK:P].bitcast(F32), 1.0), (VS[:, :, 1, QK:P].bitcast(F32), 0.0),
                                              (WOS[:, D:OW].bitcast(F32), 0.0),
                                              (WOS[QK:P, D:D + 1].bitcast(F32), 2.0 / DC))):
                if q:
                    pool.wait_ge(ones_ready, q)
                pool.memset(dst, value).then_inc(ones_ready, 1)
            pool.wait_ge(ones_ready, 6)

            def rsqrt(k):
                pool.wait_ge(var_ready[k], 1)
                pool.tensor_tensor(rstd[:, k, :], var[:, k, :], power[:], ALU.pow).then_inc(rstd_ready[k], 1)

            def add_bias(h):
                pool.wait_ge(gab_ready, 1)
                pool.wait_ge(x1n_ready, HT * (h + 1))
                for j in range(HT):
                    xt = xres[:, HT * h + j, :]
                    last = pool.tensor_tensor(xt, xt, gab[:], ALU.add)
                last.then_inc(xres_ready, 1)

            pool.wait_ge(a64_in, 16)
            pool.tensor_tensor(wsum[:], a64[:, A_KV:A_KV + D], a64[:, A_OUT:A_OUT + D], ALU.add).then_inc(wsum_ready, 1)
            rsqrt(N_LN1)
            pool.wait_ge(cst_in, 16)
            pool.tensor_copy(identb[:], ident).then_inc(bf_ready, 1)
            pool.tensor_copy(maskb[:].rearrange("p m n -> p (m n)"), cst[:, C_MASK:C_MASK + 2 * P]).then_inc(bf_ready, 1)
            rsqrt(N_LN1 + 1)
            rsqrt(N_LNC)
            add_bias(0)
            rsqrt(N_LNC + 1)
            add_bias(1)
            def low_gu(G, par, g):
                pool.wait_ge(wgu_hi, G + 1)
                pool.tensor_tensor(WS[:, par, 1, :, 0:2, :], wgroup(g)[:, :, 0:2, :],
                                   WS[:, par, 0, :, 0:2, :].bitcast(F32), ALU.subtract).then_inc(wgu_lo, 1)

            def low_d(G, par, g):
                pool.wait_ge(wd_hi, G + 1)
                pool.tensor_tensor(WS[:, par, 1, :, 2, :], wgroup(g)[:, :, 2, :],
                                   WS[:, par, 0, :, 2, :].bitcast(F32), ALU.subtract).then_inc(wd_lo, 1)

            low_gu(0, 0, 0)
            low_d(0, 0, 0)
            rsqrt(N_LN2)
            for b in range(1, 2 * HT, 2):
                probs_low(pool, 1, b, b + 1)
            low_gu(1, 1, 1)
            low_d(1, 1, 1)
            for n in range(POOL_UNITS):
                G = n // 2 + 1
                if n % 2 == 0 and G > 1:
                    low_gu(G, G % 2, G)
                inter_low(pool, n, n % 2, n >= 2)
                if n % 2 and G > 1:
                    low_d(G, G % 2, G)
                if n == 3:
                    rsqrt(N_LN2 + 1)
            with pool.Fori(0, GROUPS // 2) as it:
                for par in range(2):
                    low_gu(2 * it + (GROUPS + par), par, 2 * it + par)
                    low_d(2 * it + (GROUPS + par), par, 2 * it + par)

        @block.vector
        def _(dve):
            steps = [0]

            def link(ins):
                steps[0] += 1
                ins.then_inc(chain, 1)
                dve.wait_ge(chain, steps[0])

            def layer_stats(h, k):
                tiles = range(HT * h, HT * (h + 1))
                for i in tiles:
                    dve.bn_stats(stats[:, i, :], xres[:, i, :]).then_inc(chain, 1)
                    steps[0] += 1
                dve.wait_ge(chain, steps[0])
                for i in tiles:
                    dve.bn_aggr(mv[:, i, :], stats[:, i, :]).then_inc(chain, 1)
                    steps[0] += 1
                dve.wait_ge(chain, steps[0])
                dve.tensor_scalar(var[:, k, :], mv[:, HT * h:HT * (h + 1), 1], EPS, None, ALU.add).then_inc(var_ready[k], 1)

            def stats1(h):
                dve.wait_ge(x_in[h], 16)
                layer_stats(h, N_LN1 + h)

            def norm1(h):
                dve.wait_ge(rstd_ready[N_LN1 + h], 1)
                for j in range(HT):
                    i = HT * h + j
                    dve.tensor_scalar(xn[:, h, j, :], xres[:, i, :], mv[:, i, 0:1], rstd[:, N_LN1 + h, j:j + 1],
                                      ALU.subtract, ALU.mult).then_inc(x1n_ready, 1)

            def stats2(h):
                dve.wait_ge(x1_ready, HT * (h + 1))
                layer_stats(h, N_LN2 + h)

            def norm2(h, tiles):
                dve.wait_ge(rstd_ready[N_LN2 + h], 1)
                for j in tiles:
                    i = HT * h + j
                    dve.tensor_scalar(xn[:, h, j, :].rearrange("p (e k) -> p e k", e=2),
                                      xres[:, i, :].rearrange("p (k e) -> p e k", e=2),
                                      mv[:, i, 0:1], rstd[:, N_LN2 + h, j:j + 1],
                                      ALU.subtract, ALU.mult).then_inc(x2n_ready, 1)

            def compress(h):
                dve.wait_ge(c_done, h + 1)
                link(dve.tensor_tensor(cc[:, h], bank(4 * h + 2, HT * DC).rearrange("p (j d) -> p j d", j=HT),
                                       cbias[:].unsqueeze(1).to_broadcast([P, HT, DC]), ALU.add))
                link(dve.tensor_tensor(csq[:, h], cc[:, h], cc[:, h], ALU.mult))
                link(dve.tensor_reduce(var[:, N_LNC + h, :], csq[:, h], AX_X, ALU.add))
                dve.tensor_scalar(var[:, N_LNC + h, :], var[:, N_LNC + h, :], 1.0 / DC, EPS,
                                  ALU.mult, ALU.add).then_inc(var_ready[N_LNC + h], 1)

            def normc(h):
                dve.wait_ge(rstd_ready[N_LNC + h], 1)
                dve.tensor_tensor(csq[:, h], cc[:, h], rstd[:, N_LNC + h, :].unsqueeze(2).to_broadcast([P, HT, DC]),
                                  ALU.mult).then_inc(chat_ready, 1)

            def gamma_beta(h):
                dve.wait_ge(cht_done, h + 1)
                dve.wait_ge(a32_in, 16)
                if h == 1:
                    dve.wait_ge(qkv_done, 1)
                dve.tensor_scalar(chT[:], bank(4 * h + 3, HALF, 0, DC), a32[:, B_GAMMA:B_GAMMA + 1],
                                  a32[:, B_BETA:B_BETA + 1], ALU.mult, ALU.add).then_inc(cht_ready, 1)

            def rotate(h):
                dve.wait_ge(qk_done, h + 1)
                dve.wait_ge(rope_in, 16)
                if h == 1:
                    dve.wait_ge(sel_done, 1)
                dve.tensor_tensor(prod[:], bank(4 * h), rope_sb[:, HALF * h:HALF * (h + 1)], ALU.mult).then_inc(prod_ready, 1)

            def split_v(h):
                v_ps, (v_hi, v_lo) = v_views(h)
                dve.wait_ge(v_hi_ready, h + 1)
                dve.tensor_tensor(v_lo, v_ps, v_hi.bitcast(F32), ALU.subtract).then_inc(v_ready, 1)

            def split_qk(h):
                dst = (QS[0:QK, h, :], KS[0:QK, HALF * h:HALF * (h + 1)])
                for j in range(2):
                    dve.wait_ge(qk_hi, 2 * h + j + 1)
                    dve.scalar_tensor_tensor(dst[j], qk_h[0:QK, j, :].bitcast(F32), cst[0:QK, C_QM + j:C_QM + j + 1],
                                             bank(4 * h + 2 + j, HALF, 0, QK), ALU.mult, ALU.add).then_inc(qk_ready, 1)

            def row_max(h, first, last):
                base = len(pieces(0)) * h
                for q in range(first, last):
                    j, c0, c1 = pieces(h)[q]
                    dst = nmax_p[:, j, c0 // 512:c0 // 512 + 1] if h else nmax[:, j:j + 1]
                    dve.wait_ge(s_done, base + q + 1)
                    dve.tensor_reduce(dst, bank(4 * h + q % 4, c1 - c0), AX_X, ALU.max, negate=True).then_inc(s_max, 1)
                if h and last == len(pieces(h)):
                    dve.wait_ge(s_max, base + last)
                    dve.tensor_reduce(nmax[:, HT:], nmax_p[:], AX_X, ALU.min).then_inc(nm_ready, 1)

            def out_stack(h):
                dve.wait_ge(o_hi_ready, h + 1)
                if h == 1:
                    dve.wait_ge(ao_done, HT)
                dve.scalar_tensor_tensor(OS[:], o_hi[:].bitcast(F32), cst[:, C_OM:C_OM + 1], bank(4 * h + 3),
                                         ALU.mult, ALU.add).then_inc(o_ready, 1)

            def residual1(h, tiles):
                dve.wait_ge(xres_ready, h + 1)
                for j in tiles:
                    i = HT * h + j
                    dve.wait_ge(ao_done, i + 1)
                    link(dve.reciprocal(rden[:, i:i + 1], ps[:, 4 * h + j, D:D + 1]))
                    dve.scalar_tensor_tensor(xres[:, i, :], ps[:, 4 * h + j, 0:D], rden[:, i:i + 1], xres[:, i, :],
                                             ALU.mult, ALU.add).then_inc(x1_ready, 1)

            def full_h0():
                dve.wait_ge(t2_done, 1)
                dve.wait_ge(c_done, 2)
                for e in (1, 0):
                    if e == 0:
                        dve.wait_ge(h_hi, 1)
                    dve.tensor_scalar(hfull[:, e, :], bank(e), mods[:, M_CB + e:M_CB + e + 1],
                                      mods[:, M_SB + e:M_SB + e + 1], ALU.mult, ALU.add).then_inc(h_full, 1)
                dve.wait_ge(h_full, 2)

            def h_low(h, parts):
                for e in parts:
                    dve.wait_ge(h_hi, 2 * h + e + 1)
                    dve.tensor_tensor(H[:, h, 1, e, :], hfull[:, e, :], H[:, h, 0, e, :].bitcast(F32),
                                      ALU.subtract).then_inc(h_lo, 1)

            def decode(g, first=0, last=DECODE_STEPS):
                bits = wbuf[:, g, 0, :].bitcast(I32)
                vals = dec_a[:].bitcast(F16).rearrange("p (n e) -> p n e", e=2)
                if first == 0:
                    dve.wait_ge(grp_in[g], 32)
                    if g:
                        dve.wait_ge(dec_done, g)
                for s in range(first, last):
                    if s:
                        dve.wait_ge(chain, steps[0])
                    steps[0] += s < DECODE_STEPS - 1
                    if s == 0:
                        dve.tensor_scalar(dec_a[:], bits, 0xFF, None, ALU.bitwise_and).then_inc(chain, 1)
                    elif s == 1:
                        dve.tensor_scalar(dec_b[:], dec_a[:], 4097.0, None, ALU.mult).then_inc(chain, 1)
                    elif s == 2:
                        dve.tensor_scalar(dec_a[:], dec_b[:], 0x70007, 9, ALU.bitwise_and,
                                          ALU.logical_shift_left).then_inc(chain, 1)
                    elif s == 3:
                        dve.tensor_scalar(dec_b[:], dec_b[:], 0x80008, 12, ALU.bitwise_and,
                                          ALU.logical_shift_left).then_inc(chain, 1)
                    elif s == 4:
                        dve.tensor_tensor(dec_a[:], dec_a[:], dec_b[:], ALU.bitwise_or).then_inc(chain, 1)
                    elif s == 5:
                        dve.scalar_tensor_tensor(wbuf[:, g, 0, :], vals[:, :, 0], FP16_BIAS, wbuf[:, g, 1, :],
                                                 ALU.mult, ALU.mult).then_inc(chain, 1)
                    else:
                        dve.scalar_tensor_tensor(wbuf[:, g, 1, :], vals[:, :, 1], FP16_BIAS, wbuf[:, g, 1, :],
                                                 ALU.mult, ALU.mult).then_inc(dec_done, 1)

            def decode_more(first, last):
                for s in range(first, min(last, DECODE_STEPS * (GROUPS - EARLY))):
                    decode(EARLY + s // DECODE_STEPS, s % DECODE_STEPS, s % DECODE_STEPS + 1)

            def steps_before(n):
                return STEPS_AT_START + 2 * n if n <= 3 else STEPS_AT_START + 6 + 7 * (n - 3) // 2

            def inter_full(n, b, later=True):
                dve.wait_ge(up_done, n + 1)
                dve.wait_ge(gelu_done, n + 1)
                if later:
                    dve.wait_ge(i_hi, n - 1)
                    dve.wait_ge(i_lo, n - 1)
                dve.tensor_tensor(inter[:, b, :], bank(unit_banks(n)[1]), gel[:, b, :], ALU.mult).then_inc(inter_done, 1)

            def scale_out(h):
                for j in range(HT):
                    if j < 2:
                        dve.wait_ge(half_done, h + 1)
                    else:
                        dve.wait_ge(down_done, UNITS * (h + 1))
                    src = ps[:, Y + j // 2, D * (j % 2):D * (j % 2 + 1)]
                    dve.tensor_tensor(ys[:, j, :], src, gb_b[:], ALU.mult).then_inc(ys_ready, 1)
                    if h == 1 and j:
                        residual2(h, j - 1)

            def residual2(h, j):
                xt = xres[:, HT * h + j, :]
                dve.wait_ge(ys_ready, HT * h + j + 1)
                dve.tensor_tensor(xt, ys[:, j, :], xt, ALU.add).then_inc(y_ready, 1)

            stats1(0)
            dve.wait_ge(silu_exp, 1)
            link(dve.tensor_scalar(silu_t[:, 1, :], silu_t[:, 0, :], 1.0, None, ALU.add))
            link(dve.reciprocal(silu_t[:, 2, :], silu_t[:, 1, :]))
            dve.tensor_tensor(silu[:], c_sb[:], silu_t[:, 2, :], ALU.mult).then_inc(silu_ready, 1)

            norm1(0)

            dve.wait_ge(wc_done, 1)
            wc_ps = bank(WC_B, KT * DC).rearrange("p (k d) -> p k d", k=KT)
            link(dve.tensor_reduce(wc_mean[:], wc_ps, AX_X, ALU.add))
            link(dve.tensor_scalar(wc_mean[:], wc_mean[:], 1.0 / DC, None, ALU.mult))
            link(dve.tensor_tensor(wcc[:], wc_ps, wc_mean[:].unsqueeze(2).to_broadcast([P, KT, DC]), ALU.subtract))
            dve.wait_ge(t1_done, 1)
            dve.tensor_copy(xnT[:, 1, :], bank(1)).then_inc(t1_ready, 1)

            dve.wait_ge(moda_done, 1)
            dve.tensor_copy(mods[:, M_SA:M_SA + KT], bank(MODA_B)[:, M_SA:M_SA + KT]).then_inc(sa_ready, 1)
            link(dve.tensor_scalar(mods[:, M_CA:M_CA + KT], bank(MODA_B)[:, M_CA:M_CA + KT], 1.0, None, ALU.add))
            for k in range(KT):
                dve.tensor_scalar(wcm[:, k, :], wcc[:, k, :], mods[:, M_CA + k:M_CA + k + 1], None,
                                  ALU.mult).then_inc(wcm_ready, 1)

            def gate_floor(dst, src, tmp):
                link(dve.tensor_scalar(tmp[:, 0, :], src, 0.0, 2.0, ALU.is_ge, ALU.mult))
                link(dve.tensor_scalar(tmp[:, 0, :], tmp[:, 0, :], -1.0, None, ALU.add))
                link(dve.tensor_tensor(tmp[:, 1, :], src, tmp[:, 0, :], ALU.mult))
                link(dve.scalar_tensor_tensor(dst, tmp[:, 1, :], 0.25, tmp[:, 0, :], ALU.max, ALU.mult))

            stats1(1)
            dve.wait_ge(bias_done, 1)
            link(dve.tensor_copy(cbias[:], bank(WC_B)[:, 64:64 + DC]))
            compress(0)
            norm1(1)
            normc(0)
            decode(0, 0, 1)
            gamma_beta(0)
            decode(0, 1, 4)
            rotate(0)
            dve.wait_ge(ga_done, 1)
            gate_floor(ga_b[:], bank(GA_B, D), ga_t)
            dve.wait_ge(bout_in, 16)
            dve.tensor_tensor(gab[:], ga_b[:], bout_sb[:], ALU.mult).then_inc(gab_ready, 1)
            split_v(0)
            split_qk(0)
            dve.wait_ge(wo_done, 1)
            link(dve.tensor_tensor(wo[:], bank(WO_B, D), ga_b[:], ALU.mult))
            link(dve.tensor_copy(wo_hi[:], wo[:]))
            dve.scalar_tensor_tensor(WOS[:, 0:D], wo_hi[:].bitcast(F32), cst[:, C_WM:C_WM + 1], wo[:],
                                     ALU.mult, ALU.add).then_inc(wo_ready, 1)
            decode(0, 4, 5)
            row_max(0, 0, HT)
            dve.wait_ge(modb_done, 1)
            modb = bank(GA_B)[:, D:D + M_N]
            dve.tensor_copy(mods[:, M_SB:M_SB + KT], modb[:, M_SB:M_SB + KT]).then_inc(modb_ready, 1)
            dve.tensor_scalar(mods[:, M_CB:M_CB + KT], modb[:, M_CB:M_CB + KT], 1.0, None, ALU.add).then_inc(modb_ready, 1)
            compress(1)
            decode(0, 5, 6)
            normc(1)
            decode(0, 6)
            probs_low(dve, 0, 0, 1)
            gamma_beta(1)
            probs_low(dve, 0, 1, 3)
            decode(1, 0, 2)
            decode(1, 2, 3)
            probs_low(dve, 0, 3, HT)
            decode(1, 3, 5)
            out_stack(0)
            rotate(1)
            split_v(1)
            residual1(0, range(HT - 1))
            split_qk(1)
            residual1(0, (HT - 1,))
            row_max(1, 0, len(pieces(1)))
            stats2(0)
            probs_low(dve, 1, 0, 1)
            norm2(0, range(HT))
            probs_low(dve, 1, 2, 3)
            decode(1, 5)
            full_h0()
            h_low(0, (0, 1))
            probs_low(dve, 1, 4, 5)
            decode_more(0, 4)
            probs_low(dve, 1, 6, 7)
            decode_more(4, STEPS_AT_START)

            for n in range(UNITS + 2):
                inter_full(n, n % 2, n >= 2)
                if n == 0:
                    out_stack(1)
                elif n >= POOL_UNITS:
                    if n == POOL_UNITS:
                        dve.wait_ge(i_lo, n)
                    inter_low(dve, n, n % 2)
                if n in (1, 2):
                    residual1(1, (2 * n - 2, 2 * n - 1))
                elif n == 3:
                    stats2(1)
                elif n in (H1_UNIT - 3, H1_UNIT - 2):
                    first = 2 * (n - H1_UNIT + 3)
                    norm2(1, (first, first + 1))
                elif n in (H1_UNIT + 1, H1_UNIT + 2):
                    h_low(1, (n - H1_UNIT - 1,))
                elif n == UNITS - 1:
                    gate_floor(gb_b[:], gb_b[:], ga_t)
                decode_more(steps_before(n), steps_before(n + 1))
            scale_out(0)
            for j in range(HT):
                residual2(0, j)
            with dve.Fori(0, 3) as it:
                for j in range(4):
                    n = 4 * it + (UNITS + 2 + j)
                    inter_full(n, j % 2)
                    inter_low(dve, n, j % 2)
            for n in range(2 * UNITS - 2, 2 * UNITS):
                inter_full(n, n % 2)
                inter_low(dve, n, n % 2)
            scale_out(1)
            residual2(1, HT - 1)

        @block.tensor
        def _(pe):
            def mm(o, lhsT, rhs, start=True, stop=True):
                return pe.matmul(o, lhsT, rhs, start=start, stop=stop)

            def products(o, pairs):
                for k, (a, b) in enumerate(pairs):
                    last = mm(o, a, b, k == 0, k == len(pairs) - 1)
                return last

            def mod_columns(o, vec, paired):
                for k in range(KT):
                    base = vec * D + (k if paired else k * P)
                    step = 2 if paired else 1
                    for kt in range(KT):
                        last = mm(o[:, k:k + 1], wmod_sb[:, kt, base:base + step * (P - 1) + 1:step],
                                  silu[:, kt:kt + 1], kt == 0, kt == KT - 1)
                return last

            def transpose1(h):
                pe.wait_ge(cst_in, 16)
                if h == 1:
                    pe.wait_ge(wcm_ready, KT)
                    pe.wait_ge(gab_ready, 1)
                for j in range(HT):
                    pe.wait_ge(x1n_ready, HT * h + j + 1)
                    for k in range(KT):
                        last = pe.transpose(ps[:, 4 * h + k, P * j:P * (j + 1)], xn[:, h, j, P * k:P * (k + 1)], ident)
                last.then_inc(t1_done, 1)

            def stay_warm(b, count):
                for _ in range(count):
                    mm(bank(b), idle[:, 0:P], idle[:])

            pe.wait_ge(idle_ready, 1)
            stay_warm(WC_B, 14)
            pe.wait_ge(a64_in, 16)
            for k in range(KT):
                last = mm(bank(WC_B)[:, DC * k:DC * (k + 1)], a64[:, A_KV + P * k:A_KV + P * (k + 1)],
                          a64[:, A_CMP:A_CMP + DC])
            last.then_inc(wc_done, 1)
            pe.wait_ge(wsum_ready, 1)
            mm(bank(WO_B, D), a64[:, A_LAT:A_LAT + 4 * DC], wsum[:]).then_inc(wo_done, 1)
            stay_warm(0, 3)
            transpose1(0)
            pe.wait_ge(silu_ready, 1)
            pe.wait_ge(wmod_in[0], 16)
            mod_columns(bank(MODA_B)[:, M_SA:M_SA + KT], SA, False)
            mod_columns(bank(MODA_B)[:, M_CA:M_CA + KT], CA, False).then_inc(moda_done, 1)

            def project_c(h):
                pe.wait_ge(wcm_ready, KT)
                pe.wait_ge(t1_ready, KT * (h + 1))
                for j in range(HT):
                    last = products(ps[:, 4 * h + 2, DC * j:DC * (j + 1)],
                                    [(xnT[:, k, P * j:P * (j + 1)], wcm[:, k, :]) for k in range(KT)])
                last.then_inc(c_done, 1)

            def transpose_c(h):
                pe.wait_ge(chat_ready, h + 1)
                if h == 1:
                    pe.wait_ge(wo_ready, 1)
                for j in range(HT):
                    last = pe.transpose(ps[0:DC, 4 * h + 3, P * j:P * (j + 1)], csq[:, h, j, :], ident)
                last.then_inc(cht_done, 1)

            def project_qkv(h):
                pe.wait_ge(cht_ready, h + 1)
                pe.wait_ge(a32_in, 16)
                if h == 1:
                    pe.wait_ge(modb_ready, 2)
                mm(bank(4 * h), a32[:, B_QK:B_QK + 4 * DC], chT[:]).then_inc(qk_done, 1)
                for j in range(HT):
                    last = mm(ps[:, 4 * h + 1, DC * j:DC * (j + 1)], chT[:, P * j:P * (j + 1)], a32[:, B_V:B_V + DC])
                last.then_inc(qkv_done, 1)

            def stack_qk(h):
                pe.wait_ge(prod_ready, h + 1)
                mm(bank(4 * h + 2), cst[:, C_SELQ:C_SELQ + P], prod[:])
                mm(bank(4 * h + 3), cst[:, C_SELK:C_SELK + P], prod[:]).then_inc(sel_done, 1)

            def scores(h, first, last):
                pe.wait_ge(qk_ready, 2 * (h + 1))
                pe.wait_ge(bf_ready, 2)
                pe.wait_ge(v_ready, h + 1)
                base = len(pieces(0)) * h
                for q in range(first, last):
                    j, c0, c1 = pieces(h)[q]
                    if q >= 4:
                        pe.wait_ge(s_max, base + q - 3)
                    i = HT * h + j
                    o = bank(4 * h + q % 4, c1 - c0)
                    diag = c1 == P * (i + 1)
                    last = mm(o, QS[0:QK, h, P * j:P * (j + 1)], KS[0:QK, c0:c1], True, not diag)
                    if diag:
                        last = mm(o[:, c1 - c0 - P:], identb[:], maskb[:, 0, :], False, True)
                    last.then_inc(s_done, 1)

            def max_rows(h):
                if h == 0:
                    pe.wait_ge(s_max, len(pieces(0)))
                else:
                    pe.wait_ge(nm_ready, 1)
                for j in range(HT):
                    i = HT * h + j
                    last = mm(ps[QK:P, 4 * h + 3, P * j:P * (j + 1)], nmax[:, i:i + 1].to_broadcast([P, DC]), ident)
                last.then_inc(m_done, 1)

            def key_scores(h, b, k):
                c0 = first_col(h, b)
                pe.wait_ge(m_ready, h + 1)
                pe.wait_ge(ones_ready, 6)
                if b >= 3:
                    pe.wait_ge(p_full, k - 2)
                    pe.wait_ge(p_hi, k - 2)
                diag = b >= HT * h
                last = mm(ps[:, 4 * h + b % 3, c0:HALF], KS[:, P * b:P * (b + 1)], QS[:, h, c0:], True, not diag)
                if diag:
                    last = mm(ps[:, 4 * h + b % 3, c0:c0 + P], identb[:], maskb[:, 1, :], False, True)
                last.then_inc(st_done, 1)

            def attend(h, b, k):
                c0 = first_col(h, b)
                pe.wait_ge(p_hi, k + 1)
                pe.wait_ge(*low_maker(k))
                end = len(blocks(h)) - 1
                for q, (v, p) in enumerate(((0, PH), (0, PL), (1, PH))):
                    last = mm(ps[:, 4 * h + 3, c0:HALF], VS[:, b, v, :], p[:, k % RING, c0:], b == 0 and q == 0, b == end and q == 2)
                last.then_inc(pv_done, 1)

            def output(h):
                pe.wait_ge(o_ready, h + 1)
                pe.wait_ge(wo_ready, 1)
                for j in range(HT):
                    mm(ps[:, 4 * h + j, 0:OW], OS[:, P * j:P * (j + 1)], WOS[:]).then_inc(ao_done, 1)

            def transpose2(h):
                for j in range(HT):
                    pe.wait_ge(x2n_ready, HT * h + j + 1)
                    for k in range(KT):
                        last = pe.transpose(ps[:, 4 * h + k, P * j:P * (j + 1)], xn[:, h, j, P * k:P * (k + 1)], ident)
                last.then_inc(t2_done, 1)

            def gate_up(n, G, h, par, e, first=False, later=True, after_own_banks=False):
                banks = unit_banks(n)
                if first:
                    pe.wait_ge(h_hi, 2 * (h + 1))
                    pe.wait_ge(h_full, 2 * (h + 1))
                if e == 0:
                    pe.wait_ge(wgu_hi, G + 1)
                    pe.wait_ge(wgu_lo, G + 1)
                for m, (dst, done) in enumerate(zip(banks, (gate_done, up_done))):
                    if later:
                        pe.wait_ge((gelu_done, inter_done)[m], 1 if after_own_banks else n)
                    for q, (a, b) in enumerate(((0, 0), (1, 0), (0, 1))):
                        if first and b and m == 0:
                            pe.wait_ge(h_lo, 2 * (h + 1))
                        for k in range(2):
                            last = mm(bank(dst), WS[:, par, a, k, m, P * e:P * (e + 1)], H[:, h, b, k, :],
                                      q == k == 0, q == 2 and k == 1)
                    last.then_inc(done, 1)

            def down(n, G, h, par, e, first=False, last=False, any_h=None):
                pe.wait_ge(i_hi, n + 1)
                if e == 0:
                    pe.wait_ge(wd_hi, G + 1)
                    pe.wait_ge(wd_lo, G + 1)
                if first and h == 0:
                    pe.wait_ge(gelu_done, 2)
                    pe.wait_ge(inter_done, 2)
                elif first:
                    pe.wait_ge(ys_ready, HT)
                for m in range(2):
                    for q, (a, b) in enumerate(((0, 0), (1, 0), (0, 1))):
                        if b and m == 0:
                            pe.wait_ge(i_lo, n + 1)
                        for j in range(2):
                            ins = mm(ps[:, Y + m, D * j:D * (j + 1)], IS[:, e, b, P * (2 * m + j):P * (2 * m + j + 1)],
                                     WS[:, par, a, e, 2, :], first and q == j == 0, last and q == 2 and j == 1)
                    if last and m == 0:
                        ins.then_inc(half_done, 1)
                ins.then_inc(down_done, 1)

            pe.wait_ge(sa_ready, 1)
            products(bank(WC_B)[:, 64:64 + DC], [(mods[:, M_SA + k:M_SA + k + 1].to_broadcast([P, P]), wcc[:, k, :])
                                               for k in range(KT)]).then_inc(bias_done, 1)
            project_c(0)
            pe.wait_ge(wmod_in[1], 16)
            products(bank(GA_B, D), [(silu[:, k:k + 1].to_broadcast([P, P]), wmod_sb[:, k, GA * D:(GA + 1) * D])
                                   for k in range(KT)]).then_inc(ga_done, 1)
            stay_warm(3, 4)
            transpose_c(0)
            stay_warm(0, 3)
            project_qkv(0)
            stack_qk(0)
            transpose1(1)
            stay_warm(0, 2)
            scores(0, 0, HT)
            pe.wait_ge(t1_ready, 2 * KT)
            for m, vec in ((M_SB, SB), (M_CB, CB)):
                last = mod_columns(bank(GA_B)[:, D + m:D + m + KT], vec, True)
            last.then_inc(modb_done, 1)
            project_c(1)
            max_rows(0)
            key_scores(0, 0, 0)
            key_scores(0, 1, 1)
            transpose_c(1)
            key_scores(0, 2, 2)
            attend(0, 0, 0)
            key_scores(0, 3, 3)
            stay_warm(4, 3)
            attend(0, 1, 1)
            attend(0, 2, 2)
            attend(0, 3, 3)
            project_qkv(1)
            output(0)
            stay_warm(6, 3)
            stack_qk(1)
            stay_warm(4, 10)
            scores(1, 0, len(pieces(1)))
            pe.wait_ge(x1_ready, HT)
            products(bank(3, D), [(silu[:, k:k + 1].to_broadcast([P, P]), wmod_sb[:, k, GB * D:(GB + 1) * D])
                                  for k in range(KT)]).then_inc(gb_done, 1)
            max_rows(1)
            stay_warm(4, 4)
            for b, k in blocks(1):
                key_scores(1, b, k)
                if b == 2 * HT - 2:
                    gate_up(0, 0, 0, 0, 0, first=True, later=False)
                if b >= 2:
                    attend(1, b - 2, k - 2)
                if b == H0_BLOCK - 1:
                    transpose2(0)
            pe.wait_ge(gb_out, 1)
            gate_up(1, 0, 0, 0, 1, later=False)
            attend(1, b - 1, k - 1)
            attend(1, b, k)

            for n in range(2, UNITS + 3):
                gate_up(n, n // 2, n // UNITS, n // 2 % 2, n % 2, first=n == UNITS, after_own_banks=n == 2)
                if n == 2:
                    output(1)
                elif n == H1_UNIT:
                    transpose2(1)
                d = n - 2
                down(d, d // 2, d // UNITS, d // 2 % 2, d % 2, first=d % UNITS == 0, last=d == UNITS - 1)
            with pe.Fori(0, 3) as it:
                for j in range(4):
                    u, d = 3 + j, 1 + j
                    gate_up(4 * it + (UNITS + u), 2 * it + (GROUPS + u // 2), 1, u // 2 % 2, u % 2)
                    down(4 * it + (UNITS + d), 2 * it + (GROUPS + d // 2), 1, d // 2 % 2, d % 2)
            n = 2 * UNITS - 1
            gate_up(n, n // 2, 1, n // 2 % 2, 1)
            for d in (n - 2, n - 1, n):
                down(d, d // 2, 1, d // 2 % 2, d % 2, last=d == n)


def kernel(**inputs):
    import concourse.bacc as bacc
    from concourse.bass_utils import run_bass_kernel_spmd as run

    a = {k: np.asarray(v) for k, v in inputs.items()}
    f32 = np.float32

    consts = np.zeros((P, C_N), f32)
    eye = np.eye(P, dtype=f32)
    consts[:, C_ID:C_ID + P] = eye
    for r in range(3):
        for d in range(DC):
            consts[d, C_SELQ + DC * r + d] = consts[2 * DC + d, C_SELQ + DC * r + d] = 1
            consts[DC + d, C_SELK + DC * r + d] = consts[3 * DC + d, C_SELK + DC * r + d] = 1
    consts[:, C_MASK:C_MASK + P] = np.triu(np.full((P, P), -1e30, f32), 1)
    consts[:, C_MASKT:C_MASKT + P] = np.tril(np.full((P, P), -1e30, f32), -1)
    consts[2 * DC:QK, C_QM] = -1
    consts[DC:2 * DC, C_KM] = -1
    consts[DC:2 * DC, C_OM] = -1
    consts[QK + DC // 2:, C_OM] = -1
    consts[2 * DC:QK, C_WM] = -1
    inv_freq = f32(1) / np.power(f32(10000.0), np.arange(0, DC, 2, dtype=f32) / f32(DC))
    angle = (np.arange(T, dtype=f32)[:, None] * inv_freq[None]).T
    cos, sin = np.cos(angle), np.sin(angle)
    rope = np.ascontiguousarray(np.concatenate([cos] * 4 + [-sin, sin] * 2, 0).astype(f32))

    rolled = lambda w: np.concatenate([w[DC // 2:], w[:DC // 2]], 0)
    wq, wkv = a["L0_attn_W_q_comp"], a["L0_attn_W_kv_comp"]
    wk, wv = wkv[:DC], wkv[DC:]
    attn64 = np.ascontiguousarray(np.concatenate([
        a["L0_attn_W_to_kv"], a["L0_attn_W_out_res"].T] + [a["L0_attn_W_comp2lat"]] * 3 + [
        np.zeros((DLAT, DC), f32), a["L0_attn_W_compress"].T], 1))
    attn32 = np.ascontiguousarray(np.concatenate([
        wq.T, wk.T, rolled(wq).T, rolled(wk).T, wv.T, a["L0_attn_ln_gamma"][:, None], a["L0_attn_ln_beta"][:, None]], 1))

    def by_group(w):
        k = w.shape[1]
        return w.reshape(GROUPS, P, 2, k).transpose(0, 3, 2, 1).reshape(GROUPS, k, 2 * P)

    def down_by_group(w):
        return w.T.reshape(GROUPS, -1, D)

    packed = np.ascontiguousarray(np.concatenate([
        by_group(a["L0_ffn_gate_W_packed"]), by_group(a["L0_ffn_up_W_packed"]),
        down_by_group(a["L0_ffn_down_W_packed"])], 2))
    scales = np.ascontiguousarray(np.concatenate([
        by_group(a["L0_ffn_gate_scales"]), by_group(a["L0_ffn_up_scales"]),
        down_by_group(a["L0_ffn_down_scales"])], 2))

    arrays = {
        "x": a["L0_attn_x"], "wmod": a["L0_wmod"],
        "c_col": np.ascontiguousarray(a["L0_c"].reshape(KT, P).T),
        "attn64": attn64, "attn32": attn32, "b_out": a["L0_attn_b_out_res"],
        "consts": consts, "rope": rope, "packed": packed, "scales": scales,
    }
    nc = bacc.Bacc("TRN2", target_bir_lowering=False, num_devices=1)
    ins = {k: np.ascontiguousarray(v) for k, v in arrays.items()}
    args = [nc.dram_tensor(k, v.shape, mybir.dt.from_np(v.dtype), kind="ExternalInput").ap() for k, v in ins.items()]
    out = nc.dram_tensor("out", (1, T, D), F32, kind="ExternalOutput").ap()
    build_block(nc, *args, out)
    return run(nc, [ins], core_ids=[0]).results[0]["out"]
```
